# Optimizing a Trainium2 kernel written in Bass

```python
import numpy as np
import jax
import jax.numpy as jnp

def _softmax(x, axis=-1):
    return jax.nn.softmax(x, axis=axis)

def _gelu(x):
    return jax.nn.gelu(x, approximate=True)

def _silu(x):
    return jax.nn.silu(x)

def _sigmoid(x):
    return jax.nn.sigmoid(x)

def _layernorm(x, axis=-1, eps=1e-05):
    m = jnp.mean(x, axis=axis, keepdims=True)
    v = jnp.var(x, axis=axis, keepdims=True)
    return (x - m) / jnp.sqrt(v + eps)

def _scatter_add(tgt, idx, src, axis=0):
    return tgt.at[idx].add(src)

def _segment_sum(src, seg, n):
    return jax.ops.segment_sum(src, seg, n)
kernel_name = 'mk_dlrm_tower_d1_rec_r8_521570'

def setup_inputs(seed: int=0):
    np.random.seed(seed)
    _w = jnp.asarray

    def _rec_inputs():
        import jax
        import jax.numpy as jnp
        _tk = jax.random.key(seed)
        ids = jnp.stack([jax.random.randint(jax.random.fold_in(_tk, 200 + f), (2048,), 0, v, jnp.int32) for f, v in enumerate([125000, 1250, 12500, 1000, 1250, 12500, 12500, 12500, 1000, 1250, 1000, 12500, 1000, 1250, 1000, 1000, 1250, 12500, 1250, 12500, 1250, 1000, 12500, 1250, 1250, 1250])], axis=1)
        tbl_0 = 0.05 * jax.random.normal(jax.random.fold_in(_tk, 500 + 0), (125000, 128), jnp.float32)
        tbl_1 = 0.05 * jax.random.normal(jax.random.fold_in(_tk, 500 + 1), (1250, 128), jnp.float32)
        tbl_2 = 0.05 * jax.random.normal(jax.random.fold_in(_tk, 500 + 2), (12500, 128), jnp.float32)
        tbl_3 = 0.05 * jax.random.normal(jax.random.fold_in(_tk, 500 + 3), (1000, 128), jnp.float32)
        tbl_4 = 0.05 * jax.random.normal(jax.random.fold_in(_tk, 500 + 4), (1250, 128), jnp.float32)
        tbl_5 = 0.05 * jax.random.normal(jax.random.fold_in(_tk, 500 + 5), (12500, 128), jnp.float32)
        tbl_6 = 0.05 * jax.random.normal(jax.random.fold_in(_tk, 500 + 6), (12500, 128), jnp.float32)
        tbl_7 = 0.05 * jax.random.normal(jax.random.fold_in(_tk, 500 + 7), (12500, 128), jnp.float32)
        tbl_8 = 0.05 * jax.random.normal(jax.random.fold_in(_tk, 500 + 8), (1000, 128), jnp.float32)
        tbl_9 = 0.05 * jax.random.normal(jax.random.fold_in(_tk, 500 + 9), (1250, 128), jnp.float32)
        tbl_10 = 0.05 * jax.random.normal(jax.random.fold_in(_tk, 500 + 10), (1000, 128), jnp.float32)
        tbl_11 = 0.05 * jax.random.normal(jax.random.fold_in(_tk, 500 + 11), (12500, 128), jnp.float32)
        tbl_12 = 0.05 * jax.random.normal(jax.random.fold_in(_tk, 500 + 12), (1000, 128), jnp.float32)
        tbl_13 = 0.05 * jax.random.normal(jax.random.fold_in(_tk, 500 + 13), (1250, 128), jnp.float32)
        tbl_14 = 0.05 * jax.random.normal(jax.random.fold_in(_tk, 500 + 14), (1000, 128), jnp.float32)
        tbl_15 = 0.05 * jax.random.normal(jax.random.fold_in(_tk, 500 + 15), (1000, 128), jnp.float32)
        tbl_16 = 0.05 * jax.random.normal(jax.random.fold_in(_tk, 500 + 16), (1250, 128), jnp.float32)
        tbl_17 = 0.05 * jax.random.normal(jax.random.fold_in(_tk, 500 + 17), (12500, 128), jnp.float32)
        tbl_18 = 0.05 * jax.random.normal(jax.random.fold_in(_tk, 500 + 18), (1250, 128), jnp.float32)
        tbl_19 = 0.05 * jax.random.normal(jax.random.fold_in(_tk, 500 + 19), (12500, 128), jnp.float32)
        tbl_20 = 0.05 * jax.random.normal(jax.random.fold_in(_tk, 500 + 20), (1250, 128), jnp.float32)
        tbl_21 = 0.05 * jax.random.normal(jax.random.fold_in(_tk, 500 + 21), (1000, 128), jnp.float32)
        tbl_22 = 0.05 * jax.random.normal(jax.random.fold_in(_tk, 500 + 22), (12500, 128), jnp.float32)
        tbl_23 = 0.05 * jax.random.normal(jax.random.fold_in(_tk, 500 + 23), (1250, 128), jnp.float32)
        tbl_24 = 0.05 * jax.random.normal(jax.random.fold_in(_tk, 500 + 24), (1250, 128), jnp.float32)
        tbl_25 = 0.05 * jax.random.normal(jax.random.fold_in(_tk, 500 + 25), (1250, 128), jnp.float32)
        _rk = jax.random.fold_in(_tk, 7)
        r_dense_proj = -0.000520686 + 1.00062 * jax.random.normal(jax.random.fold_in(_rk, 101), (2048, 128), jnp.float32)
        W_top1 = 0.0405887 * jax.random.normal(jax.random.fold_in(_tk, 801), (607, 512), jnp.float32)
        W_top2 = 0.0441942 * jax.random.normal(jax.random.fold_in(_tk, 802), (512, 256), jnp.float32)
        W_top3 = 0.0625 * jax.random.normal(jax.random.fold_in(_tk, 803), (256, 1), jnp.float32)
        b_top1 = jnp.zeros((512,), jnp.float32)
        b_top2 = jnp.zeros((256,), jnp.float32)
        return (r_dense_proj, ids, tbl_0, tbl_1, tbl_2, tbl_3, tbl_4, tbl_5, tbl_6, tbl_7, tbl_8, tbl_9, tbl_10, tbl_11, tbl_12, tbl_13, tbl_14, tbl_15, tbl_16, tbl_17, tbl_18, tbl_19, tbl_20, tbl_21, tbl_22, tbl_23, tbl_24, tbl_25, W_top1, b_top1, W_top2, b_top2, W_top3)
    r_dense_proj, ids, tbl_0, tbl_1, tbl_2, tbl_3, tbl_4, tbl_5, tbl_6, tbl_7, tbl_8, tbl_9, tbl_10, tbl_11, tbl_12, tbl_13, tbl_14, tbl_15, tbl_16, tbl_17, tbl_18, tbl_19, tbl_20, tbl_21, tbl_22, tbl_23, tbl_24, tbl_25, W_top1, b_top1, W_top2, b_top2, W_top3 = _rec_inputs()

    def _L0_rec_setup():
        import jax, jax.numpy as jnp
        import numpy as np
        key = jax.random.key(seed)
        k1, k2 = jax.random.split(key)
        B, N_SPARSE, D = (2048, 26, 128)
        dense_proj = jax.random.normal(k1, (B, D), dtype=jnp.float32)
        sparse_embs = jax.random.normal(k2, (B, N_SPARSE, D), dtype=jnp.float32)
        return {'dense_proj': dense_proj, 'sparse_embs': sparse_embs}
    _L0_rec_all = _L0_rec_setup()
    _L0_rec_in = {k: v for k, v in _L0_rec_all.items() if k in ()}
    del _L0_rec_all
    return {'r_dense_proj': r_dense_proj, 'ids': ids, 'tbl_0': tbl_0, 'tbl_1': tbl_1, 'tbl_2': tbl_2, 'tbl_3': tbl_3, 'tbl_4': tbl_4, 'tbl_5': tbl_5, 'tbl_6': tbl_6, 'tbl_7': tbl_7, 'tbl_8': tbl_8, 'tbl_9': tbl_9, 'tbl_10': tbl_10, 'tbl_11': tbl_11, 'tbl_12': tbl_12, 'tbl_13': tbl_13, 'tbl_14': tbl_14, 'tbl_15': tbl_15, 'tbl_16': tbl_16, 'tbl_17': tbl_17, 'tbl_18': tbl_18, 'tbl_19': tbl_19, 'tbl_20': tbl_20, 'tbl_21': tbl_21, 'tbl_22': tbl_22, 'tbl_23': tbl_23, 'tbl_24': tbl_24, 'tbl_25': tbl_25, 'W_top1': W_top1, 'b_top1': b_top1, 'W_top2': W_top2, 'b_top2': b_top2, 'W_top3': W_top3}

def reference(r_dense_proj, ids, tbl_0, tbl_1, tbl_2, tbl_3, tbl_4, tbl_5, tbl_6, tbl_7, tbl_8, tbl_9, tbl_10, tbl_11, tbl_12, tbl_13, tbl_14, tbl_15, tbl_16, tbl_17, tbl_18, tbl_19, tbl_20, tbl_21, tbl_22, tbl_23, tbl_24, tbl_25, W_top1, b_top1, W_top2, b_top2, W_top3):
    import jax
    import jax.numpy as jnp

    def _L0_rec_ref(dense_proj, sparse_embs):
        import jax, jax.numpy as jnp
        import numpy as np
        all_vecs = jnp.concatenate([dense_proj[:, None, :], sparse_embs], axis=1)
        n = all_vecs.shape[1]
        interactions = jnp.einsum('bnd,bmd->bnm', all_vecs, all_vecs)
        rows, cols = np.triu_indices(n, k=1)
        interact_flat = interactions[:, rows, cols]
        return jnp.concatenate([dense_proj, interact_flat], axis=1)
    e = jnp.stack([tbl_0[ids[:, 0]], tbl_1[ids[:, 1]], tbl_2[ids[:, 2]], tbl_3[ids[:, 3]], tbl_4[ids[:, 4]], tbl_5[ids[:, 5]], tbl_6[ids[:, 6]], tbl_7[ids[:, 7]], tbl_8[ids[:, 8]], tbl_9[ids[:, 9]], tbl_10[ids[:, 10]], tbl_11[ids[:, 11]], tbl_12[ids[:, 12]], tbl_13[ids[:, 13]], tbl_14[ids[:, 14]], tbl_15[ids[:, 15]], tbl_16[ids[:, 16]], tbl_17[ids[:, 17]], tbl_18[ids[:, 18]], tbl_19[ids[:, 19]], tbl_20[ids[:, 20]], tbl_21[ids[:, 21]], tbl_22[ids[:, 22]], tbl_23[ids[:, 23]], tbl_24[ids[:, 24]], tbl_25[ids[:, 25]]], axis=1)
    z = _L0_rec_ref(r_dense_proj, e)
    z = z.reshape(z.shape[0], -1)
    h = jnp.concatenate([z, r_dense_proj], axis=1)
    h = jnp.maximum(h @ W_top1 + b_top1, 0.0)
    h = jnp.maximum(h @ W_top2 + b_top2, 0.0)
    y = h @ W_top3
    return y

_drawn_inputs = setup_inputs


def setup_inputs(seed=0):
    import zlib

    import numpy as np

    out = dict(_drawn_inputs(seed))
    spreads = {'b_top1': (0.0, 0.1), 'b_top2': (0.0, 0.1)}
    factors = {}
    for name, (base, spread) in spreads.items():
        noise = np.random.default_rng([zlib.crc32(name.encode()), seed]).standard_normal(out[name].shape)
        drawn = base * np.exp(spread * noise) if base else spread * noise
        out[name] = jnp.asarray(drawn.astype(out[name].dtype))
    for name, factor in factors.items():
        out[name] = (out[name] * factor).astype(out[name].dtype)
    return out
```

```python
from contextlib import ExitStack

import concourse.bass as bass
from concourse import mybir

F32 = mybir.dt.float32
F32R = mybir.dt.float32r
I32 = mybir.dt.int32
ACT = mybir.ActivationFunctionType
ALU = mybir.AluOpType

P = 128
BATCH, D = 2048, 128
NT = 26
NV = NT + 1
HOT = (3, 8, 10, 12, 14, 15)
COLD = tuple(t for t in range(NT) if t not in HOT)
ROWS_HOT = 1000
KT = 8
KP = ROWS_HOT // KT
NH, NC = len(HOT), len(COLD)
CHUNK, TILES, PAIR = 512, 4, 256
CHUNKS = BATCH // CHUNK
GB = 4
TB = NC // GB
J = 4
GROUPS = CHUNK // J
GT = GROUPS // TILES
GG = 4
STEPS = GT // GG
NPAIR = NV * (NV - 1) // 2
ZK = 3
ZP = NPAIR // ZK
H1, H2 = 512, 256
M1, M2 = H1 // P, H2 // P
TRI = [range(m, min(m + 4, NV)) for m in range(1, NV, 4)]
NTRI = len(TRI)
NS = 32
HALF = KT // 2
HALVES = 2 * NH

SLOTS = (0,) + tuple(1 + t for t in HOT) + tuple(1 + t for t in COLD)


def pair_rows():
    rows = []
    for m in range(1, NV):
        for n in range(m):
            a, b = sorted((SLOTS[n], SLOTS[m]))
            rows.append(D + a * NV - a * (a + 1) // 2 + b - a - 1)
    return rows


def hot_half(s):
    return 3 * (s // 4) + s % 4 if s % 4 < 3 else None


MLP_AT = {1: ("z", 0), 2: ("z", 1), 3: ("z", 2), 5: ("h1", 0), 7: ("h1", 1), 9: ("h1", 2),
          11: ("h1", 3), 13: ("h2", 0), 14: ("h2", 1), 15: ("y", 0)}
MLP_ITEMS = list(MLP_AT.values())


def dlrm_kernel(nc, idx, ids_rows, dense_t, hot_tables, cold_tables, w1_pairs, w1_dense, b1, w2, b2, w3, out):
    ctx = ExitStack()
    with ctx:
        def sb(name, shape, dt=F32):
            return ctx.enter_context(nc.sbuf_tensor(name, shape, dt))

        def sem(name):
            return ctx.enter_context(nc.semaphore(name))

        ident = sb("ident", [P, P])
        row_no_i = sb("row_no_i", [P, KT], I32)
        row_no = sb("row_no", [P, KT])
        idx_sb = sb("idx_sb", [P, TILES, NC], I32)
        ids_b = sb("ids_b", [P, NH, PAIR], I32)
        tab_hi = sb("tab_hi", [P, NH, KT, D], F32R)
        tab_lo = sb("tab_lo", [P, NH, KT, D], F32R)
        onehot = sb("onehot", [P, 2, HALF, PAIR], F32R)
        rows = sb("rows", [P, 2, NC, D])
        X = sb("X", [P, TILES, P * NS])
        G = sb("G", [P, NV, GROUPS])
        Zt = sb("Zt", [P, J, NPAIR])
        dense_x = sb("dense_x", [P, CHUNK])
        dense_m = sb("dense_m", [P, CHUNK])
        z_hi = sb("z_hi", [P, ZK + 1, PAIR], F32R)
        z_lo = sb("z_lo", [P, ZK + 1, PAIR], F32R)
        w1_hi = sb("w1_hi", [P, ZK + 1, H1], F32R)
        w1_lo = sb("w1_lo", [P, ZK + 1, H1], F32R)
        w2_sb = sb("w2_sb", [P, M1, H2])
        w3_sb = sb("w3_sb", [P, M2])
        b1_sb = sb("b1_sb", [P, M1])
        b2_sb = sb("b2_sb", [P, M2])
        h1 = sb("h1", [P, M1, PAIR])
        h2 = sb("h2", [P, M2, PAIR])
        y_sb = sb("y_sb", [1, CHUNK])
        def hot_raw(q):
            return X[:, 2 + q // 3, (q % 3) * KT * D:(q % 3 + 1) * KT * D]
        g_flat = G[:, :, :].rearrange("p m g -> p (m g)")
        w1_raw = g_flat[:, 0:(ZK + 2) * H1].rearrange("p (k n) -> p k n", k=ZK + 2)

        ps_ids = ctx.enter_context(nc.psum_tensor("ps_ids", [P, 2, PAIR], F32))
        ps_hot = ctx.enter_context(nc.psum_tensor("ps_hot", [P, 512], F32))
        ps_xt = ctx.enter_context(nc.psum_tensor("ps_xt", [P, 2, GB * P], F32))
        ps_g = ctx.enter_context(nc.psum_tensor("ps_g", [P, 2, 512], F32))
        ps_m = ctx.enter_context(nc.psum_tensor("ps_m", [P, 2, 512], F32))

        idx_loaded = [sem(f"idx_loaded_{t}") for t in range(TILES)]
        gathered = [[sem(f"gathered_{r}_{b}") for b in range(TB)] for r in range(2)]
        ids_loaded = [sem(f"ids_loaded_{h}") for h in range(2)]
        ids_used = sem("ids_used")
        hot_loaded = [sem(f"hot_loaded_{q}") for q in range(NH)]
        slots_free = sem("slots_free")
        w1_loaded = sem("w1_loaded")
        small_loaded = sem("small_loaded")
        dense_x_loaded = sem("dense_x_loaded")
        dense_m_loaded = sem("dense_m_loaded")
        ident_zero = sem("ident_zero")
        ident_ready = sem("ident_ready")
        pad_ready = sem("pad_ready")
        iota_ready = sem("iota_ready")
        row_no_ready = sem("row_no_ready")
        hot_hi_ready = sem("hot_hi_ready")
        hot_ready = sem("hot_ready")
        wd_ready = sem("wd_ready")
        w_hi_ready = sem("w_hi_ready")
        w_ready = sem("w_ready")
        onehot_ready = sem("onehot_ready")
        onehot_used = sem("onehot_used")
        hot_in_x = sem("hot_in_x")
        dense_in_x = sem("dense_in_x")
        xt_done = sem("xt_done")
        xt_in_x = sem("xt_in_x")
        gram_done = sem("gram_done")
        gram_in_g = sem("gram_in_g")
        tri_done = sem("tri_done")
        zt_ready = sem("zt_ready")
        z_done = sem("z_done")
        z_hi_ready = sem("z_hi_ready")
        z_ready = sem("z_ready")
        zd_ready = sem("zd_ready")
        h1_done = sem("h1_done")
        h1_ready = sem("h1_ready")
        h2_done = sem("h2_done")
        h2_ready = sem("h2_ready")
        y_done = sem("y_done")
        y_ready = sem("y_ready")
        y_free = [sem(f"y_free_{u}") for u in range(2)]
        stored = [sem(f"stored_{u}") for u in range(2)]

        block = ctx.enter_context(nc.Block())

        @block.sync
        def _(sp):
            def load_ids(pair, h):
                sp.dma_start(ids_b[0:KP, 3 * h:3 * h + 3, :],
                             ids_rows[bass.ds(pair, 1), 3 * h:3 * h + 3, :].broadcast_to([KP, 3, PAIR])
                             ).then_inc(ids_loaded[h], 16)

            def store(chunk, u):
                sp.dma_start(out[bass.ds(chunk * CHUNK + u * PAIR, PAIR), :].rearrange("s o -> o s"),
                             y_sb[0:1, u * PAIR:(u + 1) * PAIR]).then_inc(stored[u], 16)

            def load_idx(k, t):
                sp.dma_start(idx_sb[:, t, :], idx[:, bass.ds(k, 1), :].rearrange("p o q -> p (o q)")
                             ).then_inc(idx_loaded[t], 16)

            for t in range(TILES):
                load_idx(t, t)
            for q in range(NH):
                sp.dma_start(hot_raw(q)[0:KP, :], hot_tables[q].rearrange("(p k) d -> p (k d)", k=KT)
                             ).then_inc(hot_loaded[q], 16)
                if q < 2:
                    load_ids(0, q)
            sp.dma_start(dense_x[:, :], dense_t[:, 0:CHUNK]).then_inc(dense_x_loaded, 16)
            sp.dma_start(w1_raw[0:ZP, 0:ZK, :], w1_pairs.rearrange("(k p) n -> p k n", p=ZP)).then_inc(w1_loaded, 16)
            sp.dma_start(w1_raw[:, ZK:ZK + 2, :], w1_dense.rearrange("(k p) n -> p k n", p=P)).then_inc(w1_loaded, 16)
            sp.dma_start(w2_sb[:, :, :], w2.rearrange("(k p) n -> p k n", p=P)).then_inc(small_loaded, 16)
            sp.dma_start(w3_sb[:, :], w3.rearrange("(k p) o -> p (k o)", p=P), allow_slow_non_contiguous=True).then_inc(small_loaded, 16)
            sp.dma_start(b1_sb[:, :], b1.rearrange("(k p) -> p k", p=P), allow_slow_non_contiguous=True).then_inc(small_loaded, 16)
            sp.dma_start(b2_sb[:, :], b2.rearrange("(k p) -> p k", p=P), allow_slow_non_contiguous=True).then_inc(small_loaded, 16)
            for u in range(2):
                sp.sem_inc(y_free[u], 1)
            for h in range(2):
                sp.wait_ge(ids_used, 3 * h + 3)
                load_ids(1, h)

            def next_idx(c, t):
                sp.wait_ge(xt_done, TB * (TILES * c + t + 1))
                load_idx(TILES * (c + 1) + t, t)

            def chunk(c, first, last):
                if not last:
                    next_idx(c, 0)
                    sp.wait_ge(dense_in_x, 4 * c + 4)
                    sp.dma_start(dense_x[:, :], dense_t[:, bass.ds((c + 1) * CHUNK, CHUNK)]).then_inc(dense_x_loaded, 16)
                    for h in range(2):
                        sp.wait_ge(ids_used, NH * (2 * c + 1) + 3 * h + 3)
                        load_ids(2 * c + 2, h)
                    next_idx(c, 1)
                if not first:
                    sp.wait_ge(y_ready, 2 * c - 1)
                    store(c - 1, 0)
                    sp.wait_ge(stored[0], 16 * c)
                    sp.sem_inc(y_free[0], 1)
                if not last:
                    next_idx(c, 2)
                    for h in range(2):
                        sp.wait_ge(ids_used, NH * (2 * c + 2) + 3 * h + 3)
                        load_ids(2 * c + 3, h)
                    next_idx(c, 3)
                if not first:
                    sp.wait_ge(zd_ready, 2 * c)
                sp.dma_start(dense_m[:, :], dense_t[:, bass.ds(c * CHUNK, CHUNK)]).then_inc(dense_m_loaded, 16)
                if not first:
                    sp.wait_ge(y_ready, 2 * c)
                    store(c - 1, 1)
                    sp.wait_ge(stored[1], 16 * c)
                    sp.sem_inc(y_free[1], 1)

            chunk(0, True, False)
            with sp.Fori(1, CHUNKS - 1) as c:
                chunk(c, False, False)
            chunk(CHUNKS - 1, False, True)
            for u in range(2):
                sp.wait_ge(y_ready, 2 * CHUNKS - 1 + u)
                store(CHUNKS - 1, u)
            for u in range(2):
                sp.wait_ge(stored[u], 16 * CHUNKS)

        @block.gpsimd
        def _(pool):
            pool.iota(row_no_i[:, :], pattern=[[1, KT]], base=0, channel_multiplier=KT).then_inc(iota_ready, 1)
            def gather_tile(c, t, first):
                k = TILES * c + t
                r = t % 2
                for q in range(NC):
                    if q % GB == 0 and not (first and t < 2):
                        pool.wait_ge(xt_done, TB * (k - 2) + q // GB + 1)
                    if q == 0:
                        pool.wait_ge(idx_loaded[t], 16 * (c + 1))
                    if q % GB == 0 and not first:
                        pool.sem_inc(slots_free, 1)
                    pool.indirect_dma_start(rows[:, r, q, :], None, cold_tables[q],
                                            bass.IndirectOffsetOnAxis(ap=idx_sb[:, t, q:q + 1], axis=0)
                                            ).then_inc(gathered[r][q // GB], 16)

            def chunk(c, first, last):
                for t in range(TILES):
                    if first and t == 0:
                        gather_tile(c, t, first)
                        pool.memset(ident[:, :], 0.0).then_inc(ident_zero, 1)
                        pool.wait_ge(ident_zero, 1)
                        pool.affine_select(out=ident[:, :], in_=ident[:, :], compare_op=ALU.not_equal, fill=1.0,
                                           base=0, pattern=[[-1, P]], channel_multiplier=1).then_inc(ident_ready, 1)
                    else:
                        gather_tile(c, t, first)

            chunk(0, True, False)
            with pool.Fori(1, CHUNKS - 1) as c:
                chunk(c, False, False)
            chunk(CHUNKS - 1, False, True)

        @block.tensor
        def _(pe):
            def hot_step(pair, half):
                q, part = half // 2, half % 2
                n = NH * pair + q
                pe.wait_ge(onehot_ready, HALVES * pair + half + 1)
                if part == 0:
                    pe.wait_ge(hot_in_x, n)
                for k in range(HALF):
                    for w in (tab_hi, tab_lo):
                        last = nc.tensor.matmul(ps_hot[:, 0:PAIR], w[0:KP, q, part * HALF + k, :],
                                                onehot[0:KP, part, k, :],
                                                start=(part == 0 and k == 0 and w is tab_hi),
                                                stop=(part == 1 and k == HALF - 1 and w is tab_lo))
                last.then_inc(onehot_used, 1)

            def turn_step(c, t, b, first_use):
                bank = (TB * t + b) % 2
                done = TB * (TILES * c + t) + b
                pe.wait_ge(gathered[t % 2][b], 16 * GB * (2 * c + t // 2 + 1))
                if not first_use:
                    pe.wait_ge(xt_in_x, done - 1)
                for i in range(GB):
                    last = nc.tensor.transpose(ps_xt[:, bank, i * P:(i + 1) * P], rows[:, t % 2, GB * b + i, :],
                                               ident[:, :])
                last.then_inc(xt_done, 1)

            def gram_step(c, t, b, first_use):
                k = TILES * c + t
                bank = b % 2
                if b == 0:
                    pe.wait_ge(hot_in_x, NH * (2 * c + t // 2 + 1))
                    pe.wait_ge(dense_in_x, 2 * (2 * c + t // 2 + 1))
                    pe.wait_ge(xt_in_x, TB * (k + 1))
                if not first_use:
                    pe.wait_ge(gram_in_g, STEPS * k + b - 1)
                for i in range(GG):
                    at = (GG * b + i) * J * NS
                    four = X[:, t, at:at + J * NS]
                    last = nc.tensor.matmul(ps_g[:, bank, i * J * NV:(i + 1) * J * NV], four,
                                            four.rearrange("p (j n) -> p j n", n=NS)[:, :, 0:NV], start=True, stop=True)
                last.then_inc(gram_done, 1)

            def triangle(c, first):
                pe.wait_ge(gram_in_g, STEPS * TILES * (c + 1))
                for i, ms in enumerate(TRI):
                    if i >= 2:
                        pe.wait_ge(zt_ready, NTRI * c + i - 1)
                    elif not first:
                        if i == 0:
                            pe.wait_ge(h2_ready, M2 * 2 * c)
                        else:
                            pe.wait_ge(y_ready, 2 * c)
                    for o, m in enumerate(ms):
                        last = nc.tensor.transpose(ps_m[:, i % 2, o * P:(o + 1) * P], G[:, m, :], ident[:, :])
                    last.then_inc(tri_done, 1)

            def three_passes(acc, w_hi, w_lo, x_hi, x_lo, rows_k, start, stop):
                nc.tensor.matmul(acc, w_hi(rows_k), x_hi(rows_k), start=start, stop=False)
                nc.tensor.matmul(acc, w_hi(rows_k), x_lo(rows_k), start=False, stop=False)
                return nc.tensor.matmul(acc, w_lo(rows_k), x_hi(rows_k), start=False, stop=stop)

            def mlp_item(c, u, what, i):
                U = 2 * (c - 1) + u
                n = MLP_ITEMS.index((what, i))
                bank = n % 2
                if what == "z":
                    pe.wait_ge(zt_ready, NTRI * c)
                    if i == 0 and u == 1:
                        pe.wait_ge(h2_ready, M2 * U)
                    elif i == 1 and u == 1:
                        pe.wait_ge(y_ready, U)
                    elif i == 2:
                        pe.wait_ge(z_ready, ZK * U + 1)
                    for jj in range(2):
                        last = nc.tensor.transpose(ps_m[0:ZP, bank, jj * P:(jj + 1) * P],
                                                   Zt[:, 2 * u + jj, i * ZP:(i + 1) * ZP], ident[:, :])
                    last.then_inc(z_done, 1)
                elif what == "h1":
                    pe.wait_ge(z_ready, ZK * U + ZK)
                    pe.wait_ge(zd_ready, U + 1)
                    if i >= 2:
                        pe.wait_ge(h1_ready, M1 * U + i - 1)
                    cols = slice(i * P, (i + 1) * P)
                    for k in (ZK, 0, 1, 2):
                        kp = P if k == ZK else ZP
                        last = three_passes(ps_m[:, bank, 0:PAIR],
                                            lambda r: w1_hi[0:r, k, cols], lambda r: w1_lo[0:r, k, cols],
                                            lambda r: z_hi[0:r, k, :], lambda r: z_lo[0:r, k, :],
                                            kp, k == ZK, k == ZK - 1)
                    last.then_inc(h1_done, 1)
                elif what == "h2":
                    pe.wait_ge(h1_ready, M1 * U + M1)
                    cols = slice(i * P, (i + 1) * P)
                    for k in range(M1):
                        last = nc.tensor.matmul(ps_m[:, bank, 0:PAIR], w2_sb[:, k, cols], h1[:, k, :],
                                                start=(k == 0), stop=(k == M1 - 1))
                    last.then_inc(h2_done, 1)
                else:
                    pe.wait_ge(h2_ready, M2 * U + M2)
                    for k in range(M2):
                        last = nc.tensor.matmul(ps_m[0:1, bank, 0:PAIR], w3_sb[:, k:k + 1], h2[:, k, :],
                                                start=(k == 0), stop=(k == M2 - 1))
                    last.then_inc(y_done, 1)

            def chunk(c, first, last):
                for t in range(TILES):
                    for b in range(STEPS):
                        s = STEPS * (t % 2) + b
                        gram_step(c, t, b, first and t == 0 and b < 2)
                        turn = b - (STEPS - TB)
                        if turn >= 0 and not (last and t == TILES - 1):
                            if t == TILES - 1:
                                turn_step(c + 1, 0, turn, False)
                            else:
                                turn_step(c, t + 1, turn, False)
                        if hot_half(s) is not None and not (last and t >= 2):
                            hot_step(2 * c + 1 + t // 2, hot_half(s))
                        if not first and s in MLP_AT:
                            mlp_item(c, t // 2, *MLP_AT[s])
                triangle(c, first)

            for half in range(HALVES):
                if half % 2 == 0:
                    pe.wait_ge(hot_ready, half // 2 + 1)
                hot_step(0, half)
            pe.wait_ge(ident_ready, 1)
            for b in range(TB):
                turn_step(0, 0, b, b < 2)
            pe.wait_ge(pad_ready, 1)
            chunk(0, True, False)
            pe.wait_ge(w_ready, 1)
            pe.wait_ge(small_loaded, 64)
            with pe.Fori(1, CHUNKS - 1) as c:
                chunk(c, False, False)
            chunk(CHUNKS - 1, False, True)
            for u in range(2):
                for what, i in MLP_ITEMS:
                    mlp_item(CHUNKS, u, what, i)

        @block.scalar
        def _(act):
            def pair_in_x(c, h):
                return X[:, 2 * h:2 * h + 2, :].rearrange("p t (s n) -> p t s n", n=NS)

            def hot_evac(c, h, pair, q):
                act.wait_ge(onehot_used, HALVES * pair + 2 * q + 2)
                if q == 0:
                    act.wait_ge(dense_x_loaded, 16 * (c + 1))
                    for t in range(2):
                        nc.scalar.copy(
                            pair_in_x(c, h)[:, t, :, 0].rearrange("p (g j) -> p g j", j=J),
                            dense_x[:, :].rearrange("p (j g) -> p g j", j=J)[:, GT * (2 * h + t):GT * (2 * h + t + 1), :])\
                          .then_inc(dense_in_x, 1)
                nc.scalar.copy(pair_in_x(c, h)[:, :, :, 1 + q],
                               ps_hot[:, 0:PAIR].rearrange("p (t s) -> p t s", t=2)).then_inc(hot_in_x, 1)

            def turn_evac(c, t, b):
                act.wait_ge(xt_done, TB * (TILES * c + t) + b + 1)
                n0 = 1 + NH + GB * b
                nc.scalar.copy(X[:, t, :].rearrange("p (s n) -> p s n", n=NS)[:, :, n0:n0 + GB],
                               ps_xt[:, (TB * t + b) % 2, :].rearrange("p (n s) -> p s n", n=GB)).then_inc(xt_in_x, 1)

            def gram_evac(c, t, b):
                k = TILES * c + t
                act.wait_ge(gram_done, STEPS * k + b + 1)
                g0 = GT * t + GG * b
                for j in range(J):
                    q = slice(32 * j, 32 * j + 32)
                    last = nc.scalar.copy(
                        G[q, :, g0:g0 + GG],
                        ps_g[q, b % 2, 0:GG * J * NV].rearrange("p (i m) -> p m i", i=GG)[:, NV * j:NV * (j + 1), :])
                last.then_inc(gram_in_g, 1)

            def mlp_item(c, u, what, i):
                U = 2 * (c - 1) + u
                bank = MLP_ITEMS.index((what, i)) % 2
                if what == "z":
                    act.wait_ge(z_done, ZK * U + i + 1)
                    if i == 0:
                        act.wait_ge(dense_m_loaded, 16 * c)
                        nc.scalar.copy(z_hi[:, ZK, :], dense_m[:, u * PAIR:(u + 1) * PAIR]).then_inc(z_hi_ready, 1)
                    nc.scalar.copy(z_hi[0:ZP, i, :], ps_m[0:ZP, bank, 0:PAIR]).then_inc(z_hi_ready, 1)
                elif what == "h1":
                    act.wait_ge(h1_done, M1 * U + i + 1)
                    nc.scalar.activation(h1[:, i, :], ps_m[:, bank, 0:PAIR], ACT.Relu, bias=b1_sb[:, i:i + 1]
                                         ).then_inc(h1_ready, 1)
                elif what == "h2":
                    act.wait_ge(h2_done, M2 * U + i + 1)
                    nc.scalar.activation(h2[:, i, :], ps_m[:, bank, 0:PAIR], ACT.Relu, bias=b2_sb[:, i:i + 1]
                                         ).then_inc(h2_ready, 1)

            def chunk(c, first, last):
                if not first:
                    act.wait_ge(tri_done, NTRI * c)
                for t in range(TILES):
                    for b in range(STEPS):
                        s = STEPS * (t % 2) + b
                        gram_evac(c, t, b)
                        turn = b - (STEPS - TB)
                        if turn >= 0 and not (last and t == TILES - 1):
                            if t == TILES - 1:
                                turn_evac(c + 1, 0, turn)
                            else:
                                turn_evac(c, t + 1, turn)
                        half = hot_half(s)
                        if half is not None and half % 2 == 1 and not (last and t >= 2):
                            if t >= 2:
                                hot_evac(c + 1, 0, 2 * c + 2, half // 2)
                            else:
                                hot_evac(c, 1, 2 * c + 1, half // 2)
                        if not first and s in MLP_AT:
                            mlp_item(c, t // 2, *MLP_AT[s])

            for q in range(NH):
                act.wait_ge(hot_loaded[q], 16)
                nc.scalar.copy(tab_hi[0:KP, q, :, :].rearrange("p k d -> p (k d)"), hot_raw(q)[0:KP, :]
                               ).then_inc(hot_hi_ready, 1)
            for q in range(NH):
                hot_evac(0, 0, 0, q)
            act.wait_ge(w1_loaded, 32)
            nc.scalar.copy(w1_hi[0:ZP, 0:ZK, :], w1_raw[0:ZP, 0:ZK, :]).then_inc(w_hi_ready, 1)
            act.wait_ge(wd_ready, 1)
            nc.scalar.copy(w1_hi[:, ZK, :], w1_raw[:, ZK, :]).then_inc(w_hi_ready, 1)
            act.wait_ge(small_loaded, 64)
            for b in range(TB):
                turn_evac(0, 0, b)
            act.wait_ge(w_ready, 1)
            chunk(0, True, False)
            with act.Fori(1, CHUNKS - 1) as c:
                chunk(c, False, False)
            chunk(CHUNKS - 1, False, True)
            for u in range(2):
                for what, i in MLP_ITEMS:
                    mlp_item(CHUNKS, u, what, i)

        @block.vector
        def _(dve):
            def make_onehot(pair, half):
                q, part = half // 2, half % 2
                done = HALVES * pair + half
                if part == 0:
                    h = q // 3
                    dve.wait_ge(ids_loaded[h], 16 * (pair + 1))
                    nc.vector.tensor_copy(ps_ids[0:KP, q % 2, :], ids_b[0:KP, q, :]).then_inc(ids_used, 1)
                    dve.wait_ge(ids_used, NH * pair + q + 1)
                if not (isinstance(pair, int) and done < 2):
                    dve.wait_ge(onehot_used, done - 1)
                for k in range(HALF):
                    kk = part * HALF + k
                    last = nc.vector.tensor_scalar(onehot[0:KP, part, k, :], ps_ids[0:KP, q % 2, :],
                                                   row_no[0:KP, kk:kk + 1], None, ALU.is_equal)
                last.then_inc(onehot_ready, 1)

            def triangle(c):
                for i, ms in enumerate(TRI):
                    dve.wait_ge(tri_done, NTRI * c + i + 1)
                    for o, m in enumerate(ms):
                        off = m * (m - 1) // 2
                        last = nc.vector.tensor_copy(
                            Zt[:, :, off:off + m],
                            ps_m[:, i % 2, o * P:(o + 1) * P].rearrange("p (j n) -> p j n", j=J)[:, :, 0:m])
                    last.then_inc(zt_ready, 1)

            def mlp_item(c, u, what, i):
                U = 2 * (c - 1) + u
                bank = MLP_ITEMS.index((what, i)) % 2
                if what == "z":
                    if i == 0:
                        dve.wait_ge(z_hi_ready, (ZK + 1) * U + 1)
                        nc.vector.tensor_tensor(z_lo[:, ZK, :], dense_m[:, u * PAIR:(u + 1) * PAIR], z_hi[:, ZK, :],
                                                ALU.subtract).then_inc(zd_ready, 1)
                    dve.wait_ge(z_hi_ready, (ZK + 1) * U + 2 + i)
                    nc.vector.tensor_tensor(z_lo[0:ZP, i, :], ps_m[0:ZP, bank, 0:PAIR], z_hi[0:ZP, i, :],
                                            ALU.subtract).then_inc(z_ready, 1)
                elif what == "y":
                    dve.wait_ge(y_done, U + 1)
                    dve.wait_ge(y_free[u], c)
                    nc.vector.tensor_copy(y_sb[0:1, u * PAIR:(u + 1) * PAIR], ps_m[0:1, bank, 0:PAIR]
                                          ).then_inc(y_ready, 1)

            def chunk(c, first, last):
                for t in range(TILES):
                    for b in range(STEPS):
                        s = STEPS * (t % 2) + b
                        half = hot_half(s)
                        if half is not None and not (last and t >= 2):
                            pair = 2 * c + 1 + t // 2
                            if half + 1 < HALVES:
                                make_onehot(pair, half + 1)
                            elif not (last and t >= 1):
                                make_onehot(pair + 1, 0)
                        if not first and s in MLP_AT:
                            mlp_item(c, t // 2, *MLP_AT[s])
                triangle(c)

            dve.wait_ge(iota_ready, 1)
            nc.vector.tensor_copy(row_no[:, :], row_no_i[:, :]).then_inc(row_no_ready, 1)
            dve.wait_ge(row_no_ready, 1)
            for q in range(NH):
                if q < 2:
                    make_onehot(0, q)
                dve.wait_ge(hot_hi_ready, q + 1)
                nc.vector.tensor_tensor(tab_lo[0:KP, q, :, :].rearrange("p k d -> p (k d)"), hot_raw(q)[0:KP, :],
                                        tab_hi[0:KP, q, :, :].rearrange("p k d -> p (k d)"),
                                        ALU.subtract).then_inc(hot_ready, 1)
            for half in range(2, HALVES):
                make_onehot(0, half)
            dve.wait_ge(hot_ready, NH)
            nc.vector.memset(X[:, :, :].rearrange("p t (s n) -> p t s n", n=NS)[:, :, :, NV:NS], 0.0).then_inc(pad_ready, 1)
            dve.wait_ge(w1_loaded, 32)
            nc.vector.tensor_tensor(w1_raw[:, ZK, :], w1_raw[:, ZK, :], w1_raw[:, ZK + 1, :], ALU.add).then_inc(wd_ready, 1)
            dve.wait_ge(w_hi_ready, 1)
            nc.vector.tensor_tensor(w1_lo[0:ZP, 0:ZK, :], w1_raw[0:ZP, 0:ZK, :], w1_hi[0:ZP, 0:ZK, :], ALU.subtract)
            dve.wait_ge(w_hi_ready, 2)
            dve.wait_ge(wd_ready, 1)
            nc.vector.tensor_tensor(w1_lo[:, ZK, :], w1_raw[:, ZK, :], w1_hi[:, ZK, :], ALU.subtract).then_inc(w_ready, 1)
            make_onehot(1, 0)
            chunk(0, True, False)
            with dve.Fori(1, CHUNKS - 1) as c:
                chunk(c, False, False)
            chunk(CHUNKS - 1, False, True)
            for u in range(2):
                for what, i in MLP_ITEMS:
                    mlp_item(CHUNKS, u, what, i)


def kernel(**inputs):
    import numpy as np
    import concourse.bacc as bacc
    from concourse.bass_utils import run_bass_kernel_spmd

    a = {n: np.asarray(v) for n, v in inputs.items()}
    ids = a["ids"].reshape(CHUNKS, J, TILES, GT, NT)
    idx = np.ascontiguousarray(ids[..., list(COLD)].transpose(3, 1, 0, 2, 4)).reshape(P, CHUNKS * TILES, NC)
    ids_rows = np.ascontiguousarray(ids[..., list(HOT)].transpose(0, 4, 2, 3, 1)).reshape(CHUNKS, NH, 2, PAIR)
    ids_rows = np.ascontiguousarray(ids_rows.transpose(0, 2, 1, 3)).reshape(2 * CHUNKS, NH, PAIR)
    w1 = a["W_top1"]
    arrays = {
        "idx": idx,
        "ids_rows": ids_rows,
        "dense_t": np.ascontiguousarray(a["r_dense_proj"].T),
        "w1_pairs": np.ascontiguousarray(w1[np.array(pair_rows())]),
        "w1_dense": np.ascontiguousarray(np.concatenate([w1[0:D], w1[D + NPAIR:]])),
        "b1": a["b_top1"], "w2": a["W_top2"], "b2": a["b_top2"], "w3": a["W_top3"],
    }
    for t in HOT + COLD:
        arrays[f"tbl_{t}"] = a[f"tbl_{t}"]

    nc = bacc.Bacc("TRN2", target_bir_lowering=False, num_devices=1)
    ap = {n: nc.dram_tensor(n, v.shape, mybir.dt.from_np(v.dtype), kind="ExternalInput").ap()
          for n, v in arrays.items()}
    out = nc.dram_tensor("out", (BATCH, 1), F32, kind="ExternalOutput").ap()
    dlrm_kernel(nc, ap["idx"], ap["ids_rows"], ap["dense_t"], [ap[f"tbl_{t}"] for t in HOT],
                [ap[f"tbl_{t}"] for t in COLD], ap["w1_pairs"], ap["w1_dense"], ap["b1"], ap["w2"], ap["b2"],
                ap["w3"], out)
    r = run_bass_kernel_spmd(nc, [arrays], core_ids=[0])
    return r.results[0]["out"]
```

```python
from contextlib import ExitStack

import concourse.bass as bass
from concourse import mybir

F32 = mybir.dt.float32
F32R = mybir.dt.float32r
I32 = mybir.dt.int32
ACT = mybir.ActivationFunctionType
ALU = mybir.AluOpType

P = 128
BATCH, D = 2048, 128
NT = 26
NV = NT + 1
NM = NV - 1
NS = 32
HOT = (3, 8, 10, 12, 14, 15, 21)
COLD = tuple(t for t in range(NT) if t not in HOT)
ROWS_HOT = 1000
KT = 8
KP = ROWS_HOT // KT
NH, NC = len(HOT), len(COLD)
TILES = 2
CHUNK = TILES * P
CHUNKS = BATCH // CHUNK
GB = 4
TB = -(-NC // GB)
J = 4
GROUPS = CHUNK // J
GT = GROUPS // TILES
GG = 4
STEPS = GT // GG
GM = (J - 1) * NS + NV
HALF = KT // 2
HALVES = 2 * NH
H1, H2 = 512, 256
M1, M2 = H1 // P, H2 // P
NPAIR = NV * (NV - 1) // 2

TURNS = (NV - 1) // 2
ODD = [(n, m) for m in range(1, NV, 2) for n in range(m)]
EVEN = [(n, m) for m in range(2, NV, 2) for n in range(m)]
UP = 64
REST_ODD, REST_EVEN = len(ODD) - P, len(EVEN) - P
K3 = UP + REST_EVEN
ZW = P + K3
ZK = 3
ZROWS = (P, P, K3, P)
TRI = (range(0, 4), range(4, 7), range(7, 10), range(10, 13))

SLOTS = (0,) + tuple(1 + t for t in HOT) + tuple(1 + t for t in COLD)

TURN_AT = {STEPS - TB + b: b for b in range(TB)}
HOT_AT = {s: h for h, s in enumerate(s for s in range(2 * STEPS) if s % 8)}
MLP_ITEMS = [("z", 0), ("z", 1), ("h1", 0), ("h1", 1), ("h1", 2), ("h1", 3), ("h2", 0), ("h2", 1), ("y", 0)]
MLP_AT = (1, 2, 4, 5, 7, 8, 10, 11, 13)
MLP_AT_END = (1, 2, 3, 4, 4, 5, 5, 6, 6)
W_ITEMS = 6
W_AT = dict(zip((1, 3, 5, 8, 10, 12), range(W_ITEMS)))
MLP_BANK = {item: n % 2 for n, item in enumerate(MLP_ITEMS)}


def w1_row(pair):
    a, b = sorted((SLOTS[pair[0]], SLOTS[pair[1]]))
    return D + a * NV - a * (a + 1) // 2 + b - a - 1


def zt_blocks(i):
    low, high = i * i, i * (i + 1)
    out = [(0, 0, 2 * i + 1, low)]
    here = min(max(P - high, 0), 2 * i + 2)
    if here:
        out.append((1, 0, here, high))
    if here < 2 * i + 2:
        out.append((1, here, 2 * i + 2, high + here + UP))
    return out


def dlrm_kernel(nc, idx, ids_rows, dense_t, hot_tables, cold_tables, w1_pairs, w1_dense, b1, w2, b2, w3, out):
    ctx = ExitStack()
    with ctx:
        def sb(name, shape, dt=F32):
            return ctx.enter_context(nc.sbuf_tensor(name, shape, dt))

        def sem(name):
            return ctx.enter_context(nc.semaphore(name))

        ident = sb("ident", [P, P])
        ones = sb("ones", [P, 1])
        row_no_i = sb("row_no_i", [P, KT], I32)
        row_no = sb("row_no", [P, KT])
        idx_sb = sb("idx_sb", [P, 2, TILES, NC], I32)
        ids_b = sb("ids_b", [P, 2, CHUNK], I32)
        tab_hi = sb("tab_hi", [P, NH, KT, D], F32R)
        tab_lo = sb("tab_lo", [P, NH, KT, D], F32R)
        onehot = sb("onehot", [P, 2, HALF, CHUNK], F32R)
        rows = sb("rows", [P, TILES, NC, D])
        X = sb("X", [P, 2, TILES * P * NS])
        G = sb("G", [P, NM, GROUPS])
        Zt = sb("Zt", [P, J, ZW])
        dense_x = sb("dense_x", [P, CHUNK])
        z_hi = sb("z_hi", [P, ZK + 1, CHUNK], F32R)
        z_lo = sb("z_lo", [P, ZK + 1, CHUNK], F32R)
        w1_hi = sb("w1_hi", [P, ZK + 1, H1], F32R)
        w1_lo = sb("w1_lo", [P, ZK + 1, H1], F32R)
        w2_hi = sb("w2_hi", [P, M1, H2], F32R)
        w2_lo = sb("w2_lo", [P, M1, H2], F32R)
        w3_sb = sb("w3_sb", [P, M2])
        b1_sb = sb("b1_sb", [P, M1])
        b2_sb = sb("b2_sb", [P, M2])
        h1_f = sb("h1_f", [P, 2, CHUNK])
        h1_hi = sb("h1_hi", [P, M1, CHUNK], F32R)
        h1_lo = sb("h1_lo", [P, M1, CHUNK], F32R)
        h2 = sb("h2", [P, M2, CHUNK])
        hw = sb("hw", [P, CHUNK])
        y_sb = hw
        hot_raw = X[:, 1, 0:NH * KT * D].rearrange("p (q n) -> p q n", q=NH)
        ids_first_x = X[:, 1, NH * KT * D:(NH + 1) * KT * D].bitcast(I32).rearrange("p (q s) -> p q s", s=CHUNK)
        ids_first_g = G[:, :, :].rearrange("p m g -> p (m g)")[:, 0:(NH - 4) * CHUNK].bitcast(I32).rearrange(
            "p (q s) -> p q s", s=CHUNK)
        h1_stage = h1_f[:, :, :].rearrange("p k s -> p (k s)")
        h2_stage = h2[:, :, :].rearrange("p k s -> p (k s)")
        zt_stage = Zt[:, :, :].rearrange("p j z -> p (j z)")[:, 0:H1]
        w_raw = (h1_stage, zt_stage, h1_stage, h2_stage, zt_stage, h1_stage)

        def w_place(w1_part, w2_part, item):
            if item <= ZK:
                return w1_part[:, (ZK, 0, 1, 2)[item], :]
            k = 2 * (item - ZK - 1)
            return w2_part[:, k:k + 2, :].rearrange("p k n -> p (k n)")

        ps_ids = ctx.enter_context(nc.psum_tensor("ps_ids", [P, 2, CHUNK], F32))
        ps_hot = ctx.enter_context(nc.psum_tensor("ps_hot", [P, 512], F32))
        ps_xt = ctx.enter_context(nc.psum_tensor("ps_xt", [P, 2, 512], F32))
        ps_g = ctx.enter_context(nc.psum_tensor("ps_g", [P, 2, 512], F32))
        ps_m = ctx.enter_context(nc.psum_tensor("ps_m", [P, 2, 512], F32))

        idx_loaded = [[sem(f"idx_loaded_{x}_{t}") for t in range(TILES)] for x in range(2)]
        gathered = [[sem(f"gathered_{t}_{b}") for b in range(TB)] for t in range(TILES)]
        slots_free = sem("slots_free")
        ids_first_loaded = [sem(f"ids_first_loaded_{h}") for h in range(3)]
        ids_loaded = [sem(f"ids_loaded_{h}") for h in range(2)]
        ids_used = sem("ids_used")
        hot_loaded = [sem(f"hot_loaded_{q}") for q in range(NH)]
        w_loaded = [sem(f"w_loaded_{i}") for i in range(W_ITEMS)]
        small_loaded = sem("small_loaded")
        dense_x_loaded = sem("dense_x_loaded")
        ident_zero = sem("ident_zero")
        ident_ready = sem("ident_ready")
        ones_ready = sem("ones_ready")
        blanks_ready = sem("blanks_ready")
        iota_ready = sem("iota_ready")
        row_no_ready = sem("row_no_ready")
        hot_hi_ready = sem("hot_hi_ready")
        hot_ready = sem("hot_ready")
        wd_ready = sem("wd_ready")
        w_hi_ready = sem("w_hi_ready")
        w_ready = sem("w_ready")
        onehot_ready = sem("onehot_ready")
        onehot_used = sem("onehot_used")
        hot_in_x = sem("hot_in_x")
        dense_in_x = sem("dense_in_x")
        xt_done = sem("xt_done")
        xt_in_x = sem("xt_in_x")
        gram_done = sem("gram_done")
        gram_in_g = sem("gram_in_g")
        tri_done = sem("tri_done")
        zt_dve = sem("zt_dve")
        zt_act = sem("zt_act")
        z_done = sem("z_done")
        z_hi_ready = sem("z_hi_ready")
        z_ready = sem("z_ready")
        zd_ready = sem("zd_ready")
        h1_done = sem("h1_done")
        h1_f_ready = sem("h1_f_ready")
        h1_hi_ready = sem("h1_hi_ready")
        h1_ready = sem("h1_ready")
        h2_done = sem("h2_done")
        h2_ready = sem("h2_ready")
        hw_first = sem("hw_first")
        hw_ready = sem("hw_ready")
        y_done = sem("y_done")
        y_ready = sem("y_ready")
        stored = sem("stored")

        block = ctx.enter_context(nc.Block())

        def all_chunks(eng, chunk):
            chunk(0, 0, 0)
            with eng.Fori(0, CHUNKS // 2 - 1) as i:
                chunk(2 * i + 1, 1, i)
                chunk(2 * i + 2, 0, i + 1)
            chunk(CHUNKS - 1, 1, CHUNKS // 2 - 1)

        def mlp_items(c, s):
            if is_first(c):
                return []
            return [item for item, at in zip(MLP_ITEMS, MLP_AT_END if is_last(c) else MLP_AT) if at == s]

        def is_first(c):
            return isinstance(c, int) and c == 0

        def is_last(c):
            return isinstance(c, int) and c == CHUNKS - 1

        def ids_slot(x, n, q):
            before = NH * x + q
            return before % 2, NH * n + before // 2 + 1

        def dense_of(x):
            return X[:, x, :].rearrange("p (g j n) -> p j g n", j=J, n=NS)[:, :, :, 0]

        def split_samples(a):
            return a.rearrange("p (j g) -> p j g", j=J)

        def x_tile(x, t):
            return X[:, x, t * P * NS:(t + 1) * P * NS].rearrange("p (s n) -> p s n", n=NS)

        def tri_bank(i):
            return (ps_m[:, 1, :], ps_m[:, 0, :], ps_xt[:, 1, :], ps_xt[:, 0, :])[i]

        def pack_triangle(copy, i):
            for o, turn in enumerate(TRI[i]):
                for upper, n0, n1, col in zt_blocks(turn):
                    half = slice(UP * upper, UP * upper + GROUPS)
                    last = copy(Zt[half, :, col:col + n1 - n0],
                                tri_bank(i)[half, o * P:(o + 1) * P]
                                .rearrange("p (j n) -> p j n", j=J)[:, :, n0:n1])
            return last

        def z_parts(i, z):
            ps = ps_m[:, MLP_BANK["z", i], :].rearrange("p (j u g) -> p u j g", j=J, u=2)
            zz = z[:, :, :].rearrange("p k (j g) -> p k j g", j=J)
            if i == 0:
                return [(zz[:, upper, :, :], ps[:, upper, :, :]) for upper in range(2)]
            return [(zz[0:REST_ODD, 2, :, :], ps[0:REST_ODD, 0, :, :]), (zz[UP:K3, 2, :, :], ps[UP:K3, 1, :, :])]

        def load_w(eng, item):
            if item == 0:
                eng.dma_start(h1_stage, w1_dense[0:P, :]).then_inc(w_loaded[item], 16)
                eng.dma_start(h2_stage, w1_dense[P:2 * P, :]).then_inc(w_loaded[item], 16)
            elif item <= ZK:
                eng.dma_start(w_raw[item], w1_pairs[(item - 1) * P:item * P, :]).then_inc(w_loaded[item], 16)
            else:
                k = 2 * (item - ZK - 1)
                eng.dma_start(w_raw[item].rearrange("p (k n) -> p k n", k=2),
                              w2[k * P:(k + 2) * P, :].rearrange("(k p) n -> p k n", p=P)
                              ).then_inc(w_loaded[item], 16)

        @block.sync
        def _(sp):
            def load_idx(c, x):
                for t in range(TILES):
                    sp.dma_start(idx_sb[:, x, t, :], idx[:, bass.ds(TILES * c + t, 1), :].rearrange("p o q -> p (o q)")
                                 ).then_inc(idx_loaded[x][t], 16)

            def load_dense(c):
                sp.dma_start(dense_x[:, :], dense_t[:, bass.ds(c * CHUNK, CHUNK)]).then_inc(dense_x_loaded, 16)

            sp.sem_inc(stored, 16)
            load_idx(0, 0)
            for part, (dst, q0, q1) in enumerate(((ids_first_x[0:KP, 0:1, :], 0, 1), (ids_first_x[0:KP, 1:4, :], 1, 4),
                                                  (ids_first_g[0:KP, :, :], 4, NH))):
                sp.dma_start(dst, ids_rows[0:1, q0:q1, :].broadcast_to([KP, q1 - q0, CHUNK])
                             ).then_inc(ids_first_loaded[part], 16)
            load_dense(0)
            sp.wait_ge(hot_loaded[NH - 1], 16)
            load_w(sp, 0)
            load_w(sp, 1)
            sp.dma_start(w3_sb[:, :], w3.rearrange("(k p) o -> p (k o)", p=P), allow_slow_non_contiguous=True
                         ).then_inc(small_loaded, 16)
            sp.dma_start(b1_sb[:, :], b1.rearrange("(k p) -> p k", p=P), allow_slow_non_contiguous=True
                         ).then_inc(small_loaded, 16)
            sp.dma_start(b2_sb[:, :], b2.rearrange("(k p) -> p k", p=P), allow_slow_non_contiguous=True
                         ).then_inc(small_loaded, 16)
            def chunk(c, x, n):
                if not is_last(c):
                    for q in range(NH):
                        if not (is_first(c) and q < 2):
                            sp.wait_ge(ids_used, NH * c + q - 1)
                        slot, _ = ids_slot(x, n, q)
                        sp.dma_start(ids_b[0:KP, slot:slot + 1, :],
                                     ids_rows[bass.ds(c + 1, 1), q:q + 1, :].broadcast_to([KP, 1, CHUNK])
                                     ).then_inc(ids_loaded[slot], 16)
                        if q == 1:
                            if not is_first(c):
                                sp.wait_ge(xt_done, TB * TILES * c)
                            load_idx(c + 1, 1 - x)
                            sp.wait_ge(dense_in_x, TILES * (c + 1))
                            load_dense(c + 1)

            all_chunks(sp, chunk)
            sp.wait_ge(stored, 16 * (CHUNKS + 1))

        @block.gpsimd
        def _(pool):
            pool.iota(row_no_i[:, :], pattern=[[1, KT]], base=0, channel_multiplier=KT).then_inc(iota_ready, 1)
            pool.memset(ident[:, :], 0.0).then_inc(ident_zero, 1)
            pool.wait_ge(ident_zero, 1)
            pool.affine_select(out=ident[:, :], in_=ident[:, :], compare_op=ALU.not_equal, fill=1.0,
                               base=0, pattern=[[-1, P]], channel_multiplier=1).then_inc(ident_ready, 1)

            def chunk(c, x, n):
                for t in range(TILES):
                    for q in range(NC):
                        wait = q % GB == 0 and not is_first(c)
                        if wait:
                            pool.wait_ge(xt_done, TB * (TILES * (c - 1) + t) + q // GB + 1)
                        if q == 0:
                            pool.wait_ge(idx_loaded[x][t], 16 * (n + 1))
                        if wait:
                            pool.sem_inc(slots_free, 1)
                        pool.indirect_dma_start(rows[:, t, q, :], None, cold_tables[q],
                                                bass.IndirectOffsetOnAxis(ap=idx_sb[:, x, t, q:q + 1], axis=0)
                                                ).then_inc(gathered[t][q // GB], 16)

            all_chunks(pool, chunk)

        @block.tensor
        def _(pe):
            def hot_step(c, half):
                q, part = half // 2, half % 2
                pe.wait_ge(onehot_ready, HALVES * c + half + 1)
                if part == 0 and not (is_first(c) and q == 0):
                    pe.wait_ge(hot_in_x, NH * c + q)
                for w in (tab_hi, tab_lo):
                    if is_first(c) and part == 0:
                        pe.wait_ge(hot_hi_ready if w is tab_hi else hot_ready, q + 1)
                    for k in range(HALF):
                        last = nc.tensor.matmul(ps_hot[:, 0:CHUNK], w[0:KP, q, part * HALF + k, :],
                                                onehot[0:KP, part, k, :],
                                                start=(part == 0 and k == 0 and w is tab_hi),
                                                stop=(part == 1 and k == HALF - 1 and w is tab_lo))
                last.then_inc(onehot_used, 1)

            def turn_step(c, t, b):
                tables = range(GB * b, min(GB * (b + 1), NC))
                pe.wait_ge(gathered[t][b], 16 * len(tables) * (c + 1))
                if not (is_first(c) and TB * t + b < 2):
                    pe.wait_ge(xt_in_x, TB * (TILES * c + t) + b - 1)
                for i, q in enumerate(tables):
                    last = nc.tensor.transpose(ps_xt[:, (TB * t + b) % 2, i * P:(i + 1) * P],
                                               rows[:, t, q, :], ident[:, :])
                last.then_inc(xt_done, 1)

            def gram_step(c, x, t, b):
                k = TILES * c + t
                if b == 0:
                    pe.wait_ge(hot_in_x, NH * (c + 1))
                    pe.wait_ge(dense_in_x, TILES * (c + 1))
                    pe.wait_ge(xt_in_x, TB * (k + 1))
                if not (is_first(c) and t == 0 and b < 2):
                    pe.wait_ge(gram_in_g, STEPS * k + b - 1)
                for i in range(GG):
                    s0 = (GG * b + i) * J
                    four = x_tile(x, t)[:, s0:s0 + J, :]
                    last = nc.tensor.matmul(ps_g[0:GM, b % 2, i * J * NM:(i + 1) * J * NM],
                                            four.rearrange("p j n -> p (j n)")[:, 0:GM], four[:, :, 1:NV],
                                            start=True, stop=True)
                last.then_inc(gram_done, 1)

            def triangle(c):
                pe.wait_ge(gram_in_g, STEPS * TILES * (c + 1))
                for i, turns in enumerate(TRI):
                    if i < 2 and not is_first(c):
                        pe.wait_ge((h2_ready, y_ready)[i], (M2, 1)[i] * c)
                    elif i >= 2:
                        pe.wait_ge(xt_in_x, TB * (TILES * (c + 1) + (not is_last(c))) + i - 3)
                    for o, turn in enumerate(turns):
                        two = G[0:GM, 2 * turn:2 * turn + 2, :].rearrange("p m g -> p (m g)")
                        last = nc.tensor.transpose(tri_bank(i)[:, o * P:o * P + GM], two, ident[0:GM, 0:GM])
                    last.then_inc(tri_done, 1)

            def three_passes(acc, w_hi, w_lo, x_hi, x_lo, start, stop):
                nc.tensor.matmul(acc, w_hi, x_hi, start=start, stop=False)
                nc.tensor.matmul(acc, w_hi, x_lo, start=False, stop=False)
                return nc.tensor.matmul(acc, w_lo, x_hi, start=False, stop=stop)

            def mlp_item(u, what, i):
                bank = MLP_BANK[what, i]
                acc = ps_m[:, bank, 0:CHUNK]
                cols = slice(i * P, (i + 1) * P)
                if what == "z":
                    pe.wait_ge(zt_dve, 2 * (u + 1))
                    pe.wait_ge(zt_act, 2 * (u + 1))
                    width = (P, K3)[i]
                    for j in range(J):
                        last = nc.tensor.transpose(ps_m[0:width, bank, j * P:(j + 1) * P],
                                                   Zt[:, j, P * i:P * i + width], ident[:, :])
                    last.then_inc(z_done, 1)
                elif what == "h1":
                    if i == 0:
                        pe.wait_ge(zd_ready, u + 1)
                        pe.wait_ge(z_ready, 2 * u + 1)
                    if i >= 2:
                        pe.wait_ge(h1_f_ready, M1 * u + i - 1)
                    for k in (ZK, 0, 1, 2):
                        r = ZROWS[k]
                        if i == 0 and k == 2:
                            pe.wait_ge(z_ready, 2 * u + 2)
                        last = three_passes(acc, w1_hi[0:r, k, cols], w1_lo[0:r, k, cols], z_hi[0:r, k, :],
                                            z_lo[0:r, k, :], k == ZK, k == ZK - 1)
                    last.then_inc(h1_done, 1)
                elif what == "h2":
                    for k in range(M1):
                        if i == 0 and k in (0, M1 - 1):
                            pe.wait_ge(h1_ready, M1 * u + max(k, M1 - 2) + 1)
                        last = three_passes(acc, w2_hi[:, k, cols], w2_lo[:, k, cols], h1_hi[:, k, :],
                                            h1_lo[:, k, :], k == 0, k == M1 - 1)
                    last.then_inc(h2_done, 1)
                else:
                    pe.wait_ge(hw_ready, u + 1)
                    nc.tensor.matmul(ps_m[0:1, bank, 0:CHUNK], ones[:, :], hw[:, :],
                                     start=True, stop=True).then_inc(y_done, 1)

            def chunk(c, x, n):
                for s in range(TILES * STEPS):
                    t, b = divmod(s, STEPS)
                    gram_step(c, x, t, b)
                    if b in TURN_AT:
                        if t < TILES - 1:
                            turn_step(c, t + 1, TURN_AT[b])
                        elif not is_last(c):
                            turn_step(c + 1, 0, TURN_AT[b])
                    if s in HOT_AT and not is_last(c):
                        hot_step(c + 1, HOT_AT[s])
                    for item in mlp_items(c, s):
                        mlp_item(c - 1, *item)
                triangle(c)
                if is_first(c):
                    pe.wait_ge(w_ready, W_ITEMS)
                    pe.wait_ge(ones_ready, 1)
                    pe.wait_ge(blanks_ready, 5)

            for q in range(NH):
                hot_step(0, 2 * q)
                hot_step(0, 2 * q + 1)
                if q == 0:
                    pe.wait_ge(ident_ready, 1)
                if q < TB:
                    turn_step(0, 0, q)
            pe.wait_ge(blanks_ready, 3)
            all_chunks(pe, chunk)
            for item in MLP_ITEMS:
                mlp_item(CHUNKS - 1, *item)

        @block.scalar
        def _(act):
            def hot_evac(c, x, q, body=None):
                act.wait_ge(onehot_used, HALVES * c + 2 * q + 2)
                if q == 0:
                    act.wait_ge(dense_x_loaded, 16 * (c + 1))
                    if body is not None and not is_first(body):
                        act.wait_ge(zd_ready, body)
                    for t in range(TILES):
                        nc.scalar.copy(x_tile(x, t)[:, :, 0].rearrange("p (g j) -> p g j", j=J),
                                       dense_x[:, :].rearrange("p (j g) -> p g j", j=J)[:, GT * t:GT * (t + 1), :]
                                       ).then_inc(dense_in_x, 1)
                nc.scalar.copy(X[:, x, :].rearrange("p (s n) -> p s n", n=NS)[:, :, 1 + q],
                               ps_hot[:, 0:CHUNK]).then_inc(hot_in_x, 1)

            def turn_evac(c, x, t, b):
                act.wait_ge(xt_done, TB * (TILES * c + t) + b + 1)
                n0, n = 1 + NH + GB * b, min(GB, NC - GB * b)
                nc.scalar.copy(x_tile(x, t)[:, :, n0:n0 + n],
                               ps_xt[:, (TB * t + b) % 2, 0:n * P].rearrange("p (n s) -> p s n", n=n)
                               ).then_inc(xt_in_x, 1)

            def gram_evac(c, t, b):
                act.wait_ge(gram_done, STEPS * (TILES * c + t) + b + 1)
                g0 = GT * t + GG * b
                for j in range(J):
                    rows_j = slice(NS * j, min(NS * (j + 1), GM))
                    last = nc.scalar.copy(
                        G[rows_j, :, g0:g0 + GG],
                        ps_g[rows_j, b % 2, 0:GG * J * NM]
                        .rearrange("p (i m) -> p m i", i=GG)[:, NM * j:NM * (j + 1), :])
                last.then_inc(gram_in_g, 1)

            def mlp_item(u, x, what, i):
                bank = MLP_BANK[what, i]
                if what == "z":
                    act.wait_ge(z_done, 2 * u + i + 1)
                    if i == 0:
                        nc.scalar.copy(split_samples(z_hi[:, ZK, :]), dense_of(x)).then_inc(z_hi_ready, 1)
                    for dst, src in z_parts(i, z_hi):
                        last = nc.scalar.copy(dst, src)
                    last.then_inc(z_hi_ready, 1)
                elif what == "h1":
                    act.wait_ge(h1_done, M1 * u + i + 1)
                    if i >= 2:
                        act.wait_ge(h1_ready, M1 * u + i - 1)
                    nc.scalar.activation(h1_f[:, i % 2, :], ps_m[:, bank, 0:CHUNK], ACT.Relu,
                                         bias=b1_sb[:, i:i + 1]).then_inc(h1_f_ready, 1)
                    act.wait_ge(h1_f_ready, M1 * u + i + 1)
                    nc.scalar.copy(h1_hi[:, i, :], h1_f[:, i % 2, :]).then_inc(h1_hi_ready, 1)
                elif what == "h2":
                    act.wait_ge(h2_done, M2 * u + i + 1)
                    nc.scalar.activation(h2[:, i, :], ps_m[:, bank, 0:CHUNK], ACT.Relu,
                                         bias=b2_sb[:, i:i + 1]).then_inc(h2_ready, 1)

            def store(u):
                act.wait_ge(y_ready, u + 1)
                act.dma_start(out[bass.ds(u * CHUNK, CHUNK), :].rearrange("s o -> o s"), y_sb[0:1, :]
                              ).then_inc(stored, 16)

            def w_item(i):
                if i == 0:
                    act.wait_ge(wd_ready, 1)
                else:
                    act.wait_ge(w_loaded[i], 16)
                nc.scalar.copy(w_place(w1_hi, w2_hi, i), w_raw[i]).then_inc(w_hi_ready, 1)
                if i in (1, 2, 3):
                    act.wait_ge(w_ready, i)
                    for later in ((2, 3), (4,), (5,))[i - 1]:
                        load_w(act, later)

            def chunk(c, x, n):
                if not is_first(c):
                    act.wait_ge(tri_done, len(TRI) * c)
                for s in range(TILES * STEPS):
                    t, b = divmod(s, STEPS)
                    gram_evac(c, t, b)
                    if b in TURN_AT:
                        if t < TILES - 1:
                            turn_evac(c, x, t + 1, TURN_AT[b])
                        elif not is_last(c):
                            turn_evac(c + 1, 1 - x, 0, TURN_AT[b])
                    if s in HOT_AT and HOT_AT[s] % 2 == 1 and not is_last(c):
                        hot_evac(c + 1, 1 - x, HOT_AT[s] // 2, c)
                    if s in W_AT and is_first(c):
                        w_item(W_AT[s])
                    for item in mlp_items(c, s):
                        mlp_item(c - 1, 1 - x, *item)
                if not is_first(c):
                    store(c - 1)
                else:
                    act.wait_ge(blanks_ready, 5)
                for i in (1, 3):
                    act.wait_ge(tri_done, len(TRI) * c + i + 1)
                    pack_triangle(nc.scalar.copy, i).then_inc(zt_act, 1)

            act.wait_ge(iota_ready, 1)
            nc.scalar.copy(row_no[:, :], row_no_i[:, :]).then_inc(row_no_ready, 1)
            for q in range(NH):
                act.dma_start(hot_raw[0:KP, q, :], hot_tables[q].rearrange("(p k) d -> p (k d)", k=KT)
                              ).then_inc(hot_loaded[q], 16)
            def hot_hi(q):
                act.wait_ge(hot_loaded[q], 16)
                nc.scalar.copy(tab_hi[0:KP, q, :, :].rearrange("p k d -> p (k d)"), hot_raw[0:KP, q, :]
                               ).then_inc(hot_hi_ready, 1)

            hot_hi(0)
            hot_hi(1)
            for q in range(NH):
                if q + 2 < NH:
                    hot_hi(q + 2)
                hot_evac(0, 0, q)
                if q < TB:
                    turn_evac(0, 0, 0, q)
            act.wait_ge(small_loaded, 48)
            all_chunks(act, chunk)
            for item in MLP_ITEMS:
                mlp_item(CHUNKS - 1, 1, *item)
            store(CHUNKS - 1)

        @block.vector
        def _(dve):
            def onehot_columns(ids, part):
                for k in range(HALF):
                    kk = part * HALF + k
                    last = nc.vector.tensor_scalar(onehot[0:KP, part, k, :], ids, row_no[0:KP, kk:kk + 1], None,
                                                   ALU.is_equal)
                last.then_inc(onehot_ready, 1)

            def make_onehot(c, x, n, half):
                q, part = half // 2, half % 2
                slot, count = ids_slot(x, n, q)
                if part == 0:
                    dve.wait_ge(ids_loaded[slot], 16 * count)
                    nc.vector.tensor_copy(ps_ids[0:KP, slot, :], ids_b[0:KP, slot, :]).then_inc(ids_used, 1)
                    dve.wait_ge(ids_used, NH * (c - 1) + q + 1)
                dve.wait_ge(onehot_used, HALVES * c + half - 1)
                onehot_columns(ps_ids[0:KP, slot, :], part)

            def mlp_item(u, x, what, i):
                if what == "z":
                    if i == 0:
                        dve.wait_ge(z_hi_ready, 3 * u + 1)
                        nc.vector.tensor_tensor(split_samples(z_lo[:, ZK, :]), dense_of(x),
                                                split_samples(z_hi[:, ZK, :]), ALU.subtract).then_inc(zd_ready, 1)
                    dve.wait_ge(z_hi_ready, 3 * u + 2 + i)
                    for (lo, src), (hi, _) in zip(z_parts(i, z_lo), z_parts(i, z_hi)):
                        last = nc.vector.tensor_tensor(lo, src, hi, ALU.subtract)
                    last.then_inc(z_ready, 1)
                elif what == "h1":
                    dve.wait_ge(h1_hi_ready, M1 * u + i + 1)
                    nc.vector.tensor_tensor(h1_lo[:, i, :], h1_f[:, i % 2, :], h1_hi[:, i, :],
                                            ALU.subtract).then_inc(h1_ready, 1)
                elif what == "h2":
                    dve.wait_ge(h2_ready, M2 * u + i + 1)
                    if i == 0:
                        dve.wait_ge(stored, 16 * (u + 1))
                        nc.vector.tensor_scalar(hw[:, :], h2[:, 0, :], w3_sb[:, 0:1], None, ALU.mult
                                                ).then_inc(hw_first, 1)
                    else:
                        dve.wait_ge(hw_first, u + 1)
                        nc.vector.scalar_tensor_tensor(hw[:, :], h2[:, i, :], w3_sb[:, i:i + 1], hw[:, :],
                                                       ALU.mult, ALU.add).then_inc(hw_ready, 1)
                else:
                    dve.wait_ge(y_done, u + 1)
                    nc.vector.tensor_copy(y_sb[0:1, :], ps_m[0:1, MLP_BANK["y", 0], 0:CHUNK]).then_inc(y_ready, 1)

            def w_item(i):
                if i == 0:
                    dve.wait_ge(w_loaded[i], 32)
                    nc.vector.tensor_tensor(w_raw[0], w_raw[0], h2_stage, ALU.add).then_inc(wd_ready, 1)
                    dve.wait_ge(wd_ready, 1)
                dve.wait_ge(w_hi_ready, i + 1)
                nc.vector.tensor_tensor(w_place(w1_lo, w2_lo, i), w_raw[i], w_place(w1_hi, w2_hi, i),
                                        ALU.subtract).then_inc(w_ready, 1)
                if i == W_ITEMS - 1:
                    dve.wait_ge(w_ready, W_ITEMS)
                    nc.vector.memset(Zt[:, :, :], 0.0).then_inc(blanks_ready, 1)
                    dve.wait_ge(blanks_ready, 5)

            def pack(c):
                for i in (0, 2):
                    dve.wait_ge(tri_done, len(TRI) * c + i + 1)
                    pack_triangle(nc.vector.tensor_copy, i).then_inc(zt_dve, 1)

            def chunk(c, x, n):
                if not is_last(c):
                    make_onehot(c + 1, x, n, 0)
                    make_onehot(c + 1, x, n, 1)
                if not is_first(c):
                    pack(c - 1)
                for s in range(TILES * STEPS):
                    if HOT_AT.get(s + 2, 0) >= 2 and not is_last(c):
                        make_onehot(c + 1, x, n, HOT_AT[s + 2])
                    if s in W_AT and is_first(c):
                        w_item(W_AT[s])
                    for item in mlp_items(c, s):
                        mlp_item(c - 1, 1 - x, *item)
            def clear_blanks(x):
                nc.vector.memset(X[:, x, :].rearrange("p (s n) -> p s n", n=NS)[:, :, NV:NS], 0.0
                                 ).then_inc(blanks_ready, 1)

            nc.vector.memset(ones[:, :], 1.0).then_inc(ones_ready, 1)
            nc.vector.memset(z_hi[0:K3, 2, :].bitcast(F32), 0.0).then_inc(blanks_ready, 1)
            nc.vector.memset(z_lo[0:K3, 2, :].bitcast(F32), 0.0).then_inc(blanks_ready, 1)
            clear_blanks(0)
            dve.wait_ge(row_no_ready, 1)
            for q in range(NH):
                for part in range(2):
                    if q in (0, 1, 4) and part == 0:
                        dve.wait_ge(ids_first_loaded[(0, 1, 4).index(q)], 16)
                    if q > 0:
                        dve.wait_ge(onehot_used, 2 * q + part - 1)
                    onehot_columns((ids_first_x[0:KP, q, :] if q < 4 else ids_first_g[0:KP, q - 4, :]), part)
                dve.wait_ge(hot_hi_ready, q + 1)
                nc.vector.tensor_tensor(tab_lo[0:KP, q, :, :].rearrange("p k d -> p (k d)"), hot_raw[0:KP, q, :],
                                        tab_hi[0:KP, q, :, :].rearrange("p k d -> p (k d)"),
                                        ALU.subtract).then_inc(hot_ready, 1)
            dve.wait_ge(hot_ready, NH)
            dve.wait_ge(onehot_ready, HALVES)
            clear_blanks(1)
            dve.wait_ge(small_loaded, 48)
            all_chunks(dve, chunk)
            pack(CHUNKS - 1)
            for item in MLP_ITEMS:
                mlp_item(CHUNKS - 1, 1, *item)


def kernel(**inputs):
    import numpy as np
    import concourse.bacc as bacc
    from concourse.bass_utils import run_bass_kernel_spmd

    a = {n: np.asarray(v) for n, v in inputs.items()}
    ids = a["ids"].reshape(CHUNKS, J, TILES, GT, NT)
    idx = np.ascontiguousarray(ids[..., list(COLD)].transpose(3, 1, 0, 2, 4)).reshape(P, CHUNKS * TILES, NC)
    ids_rows = np.ascontiguousarray(ids[..., list(HOT)].transpose(0, 4, 2, 3, 1)).reshape(CHUNKS, NH, CHUNK)
    w1 = a["W_top1"]
    w1_pairs = np.zeros((ZK * P, H1), w1.dtype)
    w1_pairs[0:P] = w1[[w1_row(p) for p in ODD[:P]]]
    w1_pairs[P:2 * P] = w1[[w1_row(p) for p in EVEN[:P]]]
    w1_pairs[2 * P:2 * P + REST_ODD] = w1[[w1_row(p) for p in ODD[P:]]]
    w1_pairs[2 * P + UP:2 * P + K3] = w1[[w1_row(p) for p in EVEN[P:]]]
    arrays = {
        "idx": idx,
        "ids_rows": ids_rows,
        "dense_t": np.ascontiguousarray(a["r_dense_proj"].T),
        "w1_pairs": w1_pairs,
        "w1_dense": np.ascontiguousarray(np.concatenate([w1[0:D], w1[D + NPAIR:]])),
        "b1": a["b_top1"], "w2": a["W_top2"], "b2": a["b_top2"], "w3": a["W_top3"],
    }
    for t in HOT + COLD:
        arrays[f"tbl_{t}"] = a[f"tbl_{t}"]

    nc = bacc.Bacc("TRN2", target_bir_lowering=False, num_devices=1)
    ap = {n: nc.dram_tensor(n, v.shape, mybir.dt.from_np(v.dtype), kind="ExternalInput").ap()
          for n, v in arrays.items()}
    out = nc.dram_tensor("out", (BATCH, 1), F32, kind="ExternalOutput").ap()
    dlrm_kernel(nc, ap["idx"], ap["ids_rows"], ap["dense_t"], [ap[f"tbl_{t}"] for t in HOT],
                [ap[f"tbl_{t}"] for t in COLD], ap["w1_pairs"], ap["w1_dense"], ap["b1"], ap["w2"], ap["b2"],
                ap["w3"], out)
    r = run_bass_kernel_spmd(nc, [arrays], core_ids=[0])
    return r.results[0]["out"]
```

```python
from contextlib import ExitStack

import concourse.bass as bass
from concourse import mybir

F32 = mybir.dt.float32
F32R = mybir.dt.float32r
I32 = mybir.dt.int32
ACT = mybir.ActivationFunctionType
ALU = mybir.AluOpType

P = 128
BATCH, D = 2048, 128
NT = 26
NV = NT + 1
NM = NV - 1
NS = 32
HOT = (3, 8, 10, 12, 14, 15, 21)
COLD = tuple(t for t in range(NT) if t not in HOT)
FIRST_TURN = 2
AHEAD = 3
ROWS_HOT = 1000
KT = 8
KP = ROWS_HOT // KT
NH, NC = len(HOT), len(COLD)
TILES = 2
CHUNK = TILES * P
CHUNKS = BATCH // CHUNK
IN_X = KT * D // CHUNK
FIRST_IDS = ((0, 1), (1, 2), (2, IN_X), (IN_X, NH))
GB = 4
TB = -(-NC // GB)
J = 4
GROUPS = CHUNK // J
GT = GROUPS // TILES
GG = 4
STEPS = GT // GG
GM = (J - 1) * NS + NM
HALF = KT // 2
HALVES = 2 * NH
H1, H2 = 512, 256
M1, M2 = H1 // P, H2 // P
NPAIR = NV * (NV - 1) // 2

TURNS = (NV - 1) // 2
ODD = [(n, m) for m in range(1, NV, 2) for n in range(m)]
EVEN = [(n, m) for m in range(2, NV, 2) for n in range(m)]
UP = 64
REST_ODD, REST_EVEN = len(ODD) - P, len(EVEN) - P
K3 = UP + REST_EVEN
ZW = P + K3
ZK = 3
ZROWS = (P, P, K3, P)
TRI = (range(0, 4), range(4, 7), range(7, 10), range(10, 13))

SLOTS = (0,) + tuple(1 + t for t in HOT) + tuple(1 + t for t in COLD)

TURN_AT = {STEPS - TB - 1 + b: b for b in range(TB)}
HOT_AT = {s: h for h, s in enumerate(s for s in range(2 * STEPS) if s % 8)}
MLP_ITEMS = [("z", 0), ("z", 1), ("h1", 0), ("h1", 1), ("h1", 2), ("h1", 3), ("h2", 0), ("h2", 1), ("y", 0)]
MLP_AT = dict(zip((2, 3, 5, 6, 8, 9, 11, 12, 14), MLP_ITEMS))
MLP_AT_END = dict(zip((2, 3, 4, 5, 6), MLP_ITEMS))
DENSE_AT = 13
W_ITEMS = 6
W_AT = dict(zip((1, 3, 5, 8, 10, 12), range(W_ITEMS)))
MLP_BANK = {item: n % 2 for n, item in enumerate(MLP_ITEMS)}


def w1_row(pair):
    a, b = sorted((SLOTS[pair[0]], SLOTS[pair[1]]))
    return D + a * NV - a * (a + 1) // 2 + b - a - 1


def zt_blocks(i):
    low, high = i * i, i * (i + 1)
    out = [(0, 0, 2 * i + 1, low)]
    here = min(max(P - high, 0), 2 * i + 2)
    if here:
        out.append((1, 0, here, high))
    if here < 2 * i + 2:
        out.append((1, here, 2 * i + 2, high + here + UP))
    return out


def dlrm_kernel(nc, idx, ids_rows, dense_t, hot_tables, cold_tables, w1_pairs, w1_dense, b1, w2, b2, w3, out):
    ctx = ExitStack()
    with ctx:
        def sb(name, shape, dt=F32):
            return ctx.enter_context(nc.sbuf_tensor(name, shape, dt))

        def sem(name):
            return ctx.enter_context(nc.semaphore(name))

        ident = sb("ident", [P, P])
        ones = sb("ones", [P, 1])
        row_no_i = sb("row_no_i", [P, KT], I32)
        row_no = sb("row_no", [P, KT])
        idx_sb = sb("idx_sb", [P, 2, TILES, NC], I32)
        ids_b = sb("ids_b", [P, 2, CHUNK], I32)
        tab_hi = sb("tab_hi", [P, NH, KT, D], F32R)
        tab_lo = sb("tab_lo", [P, NH, KT, D], F32R)
        onehot = sb("onehot", [P, 2, HALF, CHUNK], F32R)
        rows = sb("rows", [P, TILES, NC, D])
        X = sb("X", [P, 2, TILES * P * NS])
        G = sb("G", [P, NM, GROUPS])
        Zt = sb("Zt", [P, J, ZW])
        dense_x = sb("dense_x", [P, CHUNK])
        z_hi = sb("z_hi", [P, ZK + 1, CHUNK], F32R)
        z_lo = sb("z_lo", [P, ZK + 1, CHUNK], F32R)
        w1_hi = sb("w1_hi", [P, ZK + 1, H1], F32R)
        w1_lo = sb("w1_lo", [P, ZK + 1, H1], F32R)
        w2_hi = sb("w2_hi", [P, M1, H2], F32R)
        w2_lo = sb("w2_lo", [P, M1, H2], F32R)
        w3_sb = sb("w3_sb", [P, M2])
        b1_sb = sb("b1_sb", [P, M1])
        b2_sb = sb("b2_sb", [P, M2])
        h1_f = sb("h1_f", [P, 2, CHUNK])
        h1_hi = sb("h1_hi", [P, M1, CHUNK], F32R)
        h1_lo = sb("h1_lo", [P, M1, CHUNK], F32R)
        h2 = sb("h2", [P, M2, CHUNK])
        hw = sb("hw", [P, CHUNK])
        y_all = sb("y_all", [P, CHUNKS * TILES])
        y_sb = sb("y_sb", [CHUNKS * TILES, P])
        hot_raw = X[:, 1, 0:NH * KT * D].rearrange("p (q n) -> p q n", q=NH)
        ids_first_x = X[:, 1, NH * KT * D:(NH + 1) * KT * D].bitcast(I32).rearrange("p (q s) -> p q s", s=CHUNK)
        ids_first_g = G[:, :, :].rearrange("p m g -> p (m g)")[:, 0:(NH - IN_X) * CHUNK].bitcast(
            I32).rearrange("p (q s) -> p q s", s=CHUNK)
        h1_stage = h1_f[:, :, :].rearrange("p k s -> p (k s)")
        h2_stage = h2[:, :, :].rearrange("p k s -> p (k s)")
        zt_stage = Zt[:, :, :].rearrange("p j z -> p (j z)")[:, 0:H1]
        w_raw = (h1_stage, zt_stage, h1_stage, h2_stage, zt_stage, h1_stage)

        def w_place(w1_part, w2_part, item):
            if item <= ZK:
                return w1_part[:, (ZK, 0, 1, 2)[item], :]
            k = 2 * (item - ZK - 1)
            return w2_part[:, k:k + 2, :].rearrange("p k n -> p (k n)")

        ps_ids = ctx.enter_context(nc.psum_tensor("ps_ids", [P, 2, CHUNK], F32))
        ps_hot = ctx.enter_context(nc.psum_tensor("ps_hot", [P, 512], F32))
        ps_xt = ctx.enter_context(nc.psum_tensor("ps_xt", [P, 2, 512], F32))
        ps_g = ctx.enter_context(nc.psum_tensor("ps_g", [P, 2, 512], F32))
        ps_m = ctx.enter_context(nc.psum_tensor("ps_m", [P, 2, 512], F32))

        idx_loaded = [[sem(f"idx_loaded_{x}_{t}") for t in range(TILES)] for x in range(2)]
        gathered = [[sem(f"gathered_{t}_{b}") for b in range(TB)] for t in range(TILES)]
        slots_free = sem("slots_free")
        ids_first_loaded = [sem(f"ids_first_loaded_{i}") for i in range(len(FIRST_IDS))]
        ids_loaded = [sem(f"ids_loaded_{h}") for h in range(2)]
        ids_used = sem("ids_used")
        hot_loaded = [sem(f"hot_loaded_{q}") for q in range(NH)]
        w_loaded = [sem(f"w_loaded_{i}") for i in range(W_ITEMS)]
        small_loaded = sem("small_loaded")
        dense_x_loaded = sem("dense_x_loaded")
        ident_zero = sem("ident_zero")
        ident_ready = sem("ident_ready")
        ones_ready = sem("ones_ready")
        blanks_ready = sem("blanks_ready")
        iota_ready = sem("iota_ready")
        row_no_ready = sem("row_no_ready")
        hot_hi_ready = sem("hot_hi_ready")
        hot_ready = sem("hot_ready")
        wd_ready = sem("wd_ready")
        w_hi_ready = sem("w_hi_ready")
        w_ready = sem("w_ready")
        onehot_ready = sem("onehot_ready")
        onehot_used = sem("onehot_used")
        hot_in_x = sem("hot_in_x")
        dense_in_x = sem("dense_in_x")
        xt_done = sem("xt_done")
        xt_in_x = sem("xt_in_x")
        gram_done = sem("gram_done")
        gram_in_g = sem("gram_in_g")
        tri_done = sem("tri_done")
        zt_dve = sem("zt_dve")
        zt_act = sem("zt_act")
        z_done = sem("z_done")
        z_hi_ready = sem("z_hi_ready")
        zd_hi_ready = sem("zd_hi_ready")
        z_ready = sem("z_ready")
        zd_ready = sem("zd_ready")
        h1_done = sem("h1_done")
        h1_f_ready = sem("h1_f_ready")
        h1_hi_ready = sem("h1_hi_ready")
        h1_ready = sem("h1_ready")
        h2_done = sem("h2_done")
        h2_ready = sem("h2_ready")
        hw_first = sem("hw_first")
        hw_ready = sem("hw_ready")
        y_done = sem("y_done")
        y_ready = sem("y_ready")
        y_turned = sem("y_turned")
        y_sb_ready = sem("y_sb_ready")
        stored = sem("stored")

        block = ctx.enter_context(nc.Block())

        def all_chunks(eng, chunk):
            chunk(0, 0, 0)
            with eng.Fori(0, CHUNKS // 2 - 1) as i:
                chunk(2 * i + 1, 1, i)
                chunk(2 * i + 2, 0, i + 1)
            chunk(CHUNKS - 1, 1, CHUNKS // 2 - 1)

        def is_first(c):
            return isinstance(c, int) and c == 0

        def is_last(c):
            return isinstance(c, int) and c == CHUNKS - 1

        def ids_slot(x, n, q):
            before = NH * x + q
            return before % 2, NH * n + before // 2 + 1

        def dense_of(x):
            return X[:, x, :].rearrange("p (g j n) -> p j g n", j=J, n=NS)[:, :, :, 0]

        def split_samples(a):
            return a.rearrange("p (j g) -> p j g", j=J)

        def x_tile(x, t):
            return X[:, x, t * P * NS:(t + 1) * P * NS].rearrange("p (s n) -> p s n", n=NS)

        hot_bank = ps_hot[:, :]
        ids_bank = ps_ids[:, :, :].rearrange("p k s -> p (k s)")

        def tri_bank(c, i):
            ab = (hot_bank, ids_bank) if is_last(c) else (ps_m[:, 1, :], ps_m[:, 0, :])
            return (*ab, ps_xt[:, 1, :], ps_xt[:, 0, :])[i]

        def mlp_bank(u, what, i):
            if is_last(u) and what == "z":
                return (ids_bank, hot_bank)[i]
            if isinstance(u, int) and u == CHUNKS - 2 and what == "y":
                return ps_xt[:, 0, :]
            return ps_m[:, MLP_BANK[what, i], :]

        def finish(mlp_item, dense_to_z, triangle):
            mlp_item(CHUNKS - 2, "h1", 3)
            dense_to_z(CHUNKS - 1, 1)
            triangle(CHUNKS - 1)
            mlp_item(CHUNKS - 2, "h2", 0)
            mlp_item(CHUNKS - 1, "z", 0)
            mlp_item(CHUNKS - 1, "z", 1)
            mlp_item(CHUNKS - 2, "h2", 1)
            mlp_item(CHUNKS - 1, "h1", 0)
            mlp_item(CHUNKS - 1, "h1", 1)
            mlp_item(CHUNKS - 2, "y", 0)
            for what, i in (("h1", 2), ("h1", 3), ("h2", 0), ("h2", 1), ("y", 0)):
                mlp_item(CHUNKS - 1, what, i)

        def mlp_at(c, s):
            return None if is_first(c) else (MLP_AT_END if is_last(c) else MLP_AT).get(s)

        def pack_triangle(copy, c, i):
            for o, turn in enumerate(TRI[i]):
                for upper, n0, n1, col in zt_blocks(turn):
                    half = slice(UP * upper, UP * upper + GROUPS)
                    last = copy(Zt[half, :, col:col + n1 - n0],
                                tri_bank(c, i)[half, o * P:(o + 1) * P]
                                .rearrange("p (j n) -> p j n", j=J)[:, :, n0:n1])
            return last

        def z_parts(u, i, z):
            ps = mlp_bank(u, "z", i).rearrange("p (j u g) -> p u j g", j=J, u=2)
            zz = z[:, :, :].rearrange("p k (j g) -> p k j g", j=J)
            if i == 0:
                return [(zz[:, 0:2, :, :], ps)]
            return [(zz[0:REST_ODD, 2, :, :], ps[0:REST_ODD, 0, :, :]), (zz[UP:K3, 2, :, :], ps[UP:K3, 1, :, :])]

        def load_w(eng, item):
            if item == 0:
                eng.dma_start(h1_stage, w1_dense[0:P, :]).then_inc(w_loaded[item], 16)
                eng.dma_start(h2_stage, w1_dense[P:2 * P, :]).then_inc(w_loaded[item], 16)
            elif item <= ZK:
                eng.dma_start(w_raw[item], w1_pairs[(item - 1) * P:item * P, :]).then_inc(w_loaded[item], 16)
            else:
                k = 2 * (item - ZK - 1)
                eng.dma_start(w_raw[item].rearrange("p (k n) -> p k n", k=2),
                              w2[k * P:(k + 2) * P, :].rearrange("(k p) n -> p k n", p=P)
                              ).then_inc(w_loaded[item], 16)

        @block.sync
        def _(sp):
            def load_idx(c, x):
                for t in range(TILES):
                    sp.dma_start(idx_sb[:, x, t, :], idx[:, bass.ds(TILES * c + t, 1), :].rearrange("p o q -> p (o q)")
                                 ).then_inc(idx_loaded[x][t], 16)

            def load_dense(c):
                sp.dma_start(dense_x[:, :], dense_t[:, bass.ds(c * CHUNK, CHUNK)]).then_inc(dense_x_loaded, 16)

            load_idx(0, 0)
            for part, (q0, q1) in enumerate(FIRST_IDS):
                dst = ids_first_x[0:KP, q0:q1, :] if q0 < IN_X else ids_first_g[0:KP, q0 - IN_X:q1 - IN_X, :]
                sp.dma_start(dst, ids_rows[0:1, q0:q1, :].broadcast_to([KP, q1 - q0, CHUNK])
                             ).then_inc(ids_first_loaded[part], 16)
            load_dense(0)
            sp.wait_ge(hot_loaded[NH - 1], 16)
            load_w(sp, 0)
            load_w(sp, 1)
            sp.dma_start(w3_sb[:, :], w3.rearrange("(k p) o -> p (k o)", p=P), allow_slow_non_contiguous=True
                         ).then_inc(small_loaded, 16)
            sp.dma_start(b1_sb[:, :], b1.rearrange("(k p) -> p k", p=P), allow_slow_non_contiguous=True
                         ).then_inc(small_loaded, 16)
            sp.dma_start(b2_sb[:, :], b2.rearrange("(k p) -> p k", p=P), allow_slow_non_contiguous=True
                         ).then_inc(small_loaded, 16)

            def chunk(c, x, n):
                if not is_last(c):
                    for q in range(NH):
                        if not (is_first(c) and q < 2):
                            sp.wait_ge(ids_used, NH * c + q - 1)
                        slot, _ = ids_slot(x, n, q)
                        sp.dma_start(ids_b[0:KP, slot:slot + 1, :],
                                     ids_rows[bass.ds(c + 1, 1), q:q + 1, :].broadcast_to([KP, 1, CHUNK])
                                     ).then_inc(ids_loaded[slot], 16)
                        if q == 1:
                            if not is_first(c):
                                sp.wait_ge(xt_done, TB * TILES * c)
                            load_idx(c + 1, 1 - x)
                            sp.wait_ge(dense_in_x, TILES * (c + 1))
                            load_dense(c + 1)

            all_chunks(sp, chunk)
            sp.wait_ge(y_sb_ready, 1)
            sp.dma_start(out.rearrange("(k p) o -> k (p o)", p=P), y_sb[:, :]).then_inc(stored, 16)
            sp.wait_ge(stored, 16)

        @block.gpsimd
        def _(pool):
            pool.iota(row_no_i[:, :], pattern=[[1, KT]], base=0, channel_multiplier=KT).then_inc(iota_ready, 1)
            pool.memset(ident[:, :], 0.0).then_inc(ident_zero, 1)
            pool.wait_ge(ident_zero, 1)
            pool.affine_select(out=ident[:, :], in_=ident[:, :], compare_op=ALU.not_equal, fill=1.0,
                               base=0, pattern=[[-1, P]], channel_multiplier=1).then_inc(ident_ready, 1)

            def chunk(c, x, n):
                for t in range(TILES):
                    for q in range(NC):
                        wait = q % GB == 0 and not is_first(c)
                        if wait:
                            pool.wait_ge(xt_done, TB * (TILES * (c - 1) + t) + q // GB + 1)
                        if q == 0:
                            pool.wait_ge(idx_loaded[x][t], 16 * (n + 1))
                        if wait:
                            pool.sem_inc(slots_free, 1)
                        pool.indirect_dma_start(rows[:, t, q, :], None, cold_tables[q],
                                                bass.IndirectOffsetOnAxis(ap=idx_sb[:, x, t, q:q + 1], axis=0)
                                                ).then_inc(gathered[t][q // GB], 16)

            all_chunks(pool, chunk)

        @block.tensor
        def _(pe):
            def hot_step(c, half):
                q, part = half // 2, half % 2
                pe.wait_ge(onehot_ready, HALVES * c + half + 1)
                if part == 0 and not (is_first(c) and q == 0):
                    pe.wait_ge(hot_in_x, NH * c + q)
                for w in (tab_hi, tab_lo):
                    if is_first(c) and part == 0:
                        pe.wait_ge(hot_hi_ready if w is tab_hi else hot_ready, q + 1)
                    for k in range(HALF):
                        last = nc.tensor.matmul(ps_hot[:, 0:CHUNK], w[0:KP, q, part * HALF + k, :],
                                                onehot[0:KP, part, k, :],
                                                start=(part == 0 and k == 0 and w is tab_hi),
                                                stop=(part == 1 and k == HALF - 1 and w is tab_lo))
                last.then_inc(onehot_used, 1)

            def turn_step(c, t, b):
                tables = range(GB * b, min(GB * (b + 1), NC))
                pe.wait_ge(gathered[t][b], 16 * len(tables) * (c + 1))
                if not (is_first(c) and TB * t + b < 2):
                    pe.wait_ge(xt_in_x, TB * (TILES * c + t) + b - 1)
                if t == 1 and b < 2 and not is_first(c):
                    pe.wait_ge((zt_act, zt_dve)[(TB + b) % 2], 2 * c)
                for i, q in enumerate(tables):
                    last = nc.tensor.transpose(ps_xt[:, (TB * t + b) % 2, i * P:(i + 1) * P],
                                               rows[:, t, q, :], ident[:, :])
                last.then_inc(xt_done, 1)

            def gram_step(c, x, t, b):
                k = TILES * c + t
                if b == 0:
                    pe.wait_ge(hot_in_x, NH * (c + 1))
                    pe.wait_ge(dense_in_x, TILES * (c + 1))
                    pe.wait_ge(xt_in_x, TB * (k + 1))
                if not (is_first(c) and t == 0 and b < 2):
                    pe.wait_ge(gram_in_g, STEPS * k + b - 1)
                for i in range(GG):
                    s0 = (GG * b + i) * J
                    four = x_tile(x, t)[:, s0:s0 + J, :]
                    last = nc.tensor.matmul(ps_g[0:GM, b % 2, i * J * NM:(i + 1) * J * NM],
                                            four.rearrange("p j n -> p (j n)")[:, 0:GM], four[:, :, 1:NV],
                                            start=True, stop=True)
                last.then_inc(gram_done, 1)

            def triangle(c):
                pe.wait_ge(gram_in_g, STEPS * TILES * (c + 1))
                for i, turns in enumerate(TRI):
                    if i < 2 and not is_first(c) and not is_last(c):
                        pe.wait_ge((h2_ready, y_ready)[i], (M2, 1)[i] * c)
                    elif i >= 2:
                        pe.wait_ge(xt_in_x, TB * (TILES * (c + 1) + (not is_last(c))) + i - 3)
                    for o, turn in enumerate(turns):
                        two = G[0:GM, 2 * turn:2 * turn + 2, :].rearrange("p m g -> p (m g)")
                        last = nc.tensor.transpose(tri_bank(c, i)[:, o * P:o * P + GM], two, ident[0:GM, 0:GM])
                    last.then_inc(tri_done, 1)

            def three_passes(acc, w_hi, w_lo, x_hi, x_lo, start, stop):
                nc.tensor.matmul(acc, w_hi, x_hi, start=start, stop=False)
                nc.tensor.matmul(acc, w_hi, x_lo, start=False, stop=False)
                return nc.tensor.matmul(acc, w_lo, x_hi, start=False, stop=stop)

            def mlp_item(u, what, i):
                bank = mlp_bank(u, what, i)
                acc = bank[:, 0:CHUNK]
                cols = slice(i * P, (i + 1) * P)
                if what == "z":
                    pe.wait_ge(zt_dve, 2 * (u + 1))
                    pe.wait_ge(zt_act, 2 * (u + 1))
                    width = (P, K3)[i]
                    for j in range(J):
                        last = nc.tensor.transpose(bank[0:width, j * P:(j + 1) * P],
                                                   Zt[:, j, P * i:P * i + width], ident[:, :])
                    last.then_inc(z_done, 1)
                elif what == "h1":
                    if i == 0:
                        pe.wait_ge(zd_ready, u + 1)
                        pe.wait_ge(z_ready, 2 * u + 1)
                    if i < 2 and is_last(u):
                        pe.wait_ge(h2_ready, M2 * u - 1 + i)
                    if i >= 2:
                        pe.wait_ge(h1_f_ready, M1 * u + i - 1)
                    for k in (ZK, 0, 1, 2):
                        r = ZROWS[k]
                        if i == 0 and k == 2:
                            pe.wait_ge(z_ready, 2 * u + 2)
                        last = three_passes(acc, w1_hi[0:r, k, cols], w1_lo[0:r, k, cols], z_hi[0:r, k, :],
                                            z_lo[0:r, k, :], k == ZK, k == ZK - 1)
                    last.then_inc(h1_done, 1)
                elif what == "h2":
                    for k in range(M1):
                        if i == 0 and k in (0, M1 - 1):
                            pe.wait_ge(h1_ready, M1 * u + max(k, M1 - 2) + 1)
                        last = three_passes(acc, w2_hi[:, k, cols], w2_lo[:, k, cols], h1_hi[:, k, :],
                                            h1_lo[:, k, :], k == 0, k == M1 - 1)
                    last.then_inc(h2_done, 1)
                else:
                    pe.wait_ge(hw_ready, u + 1)
                    for h in range(TILES):
                        last = nc.tensor.matmul(bank[:, h:h + 1], hw[:, h * P:(h + 1) * P], ones[:, :],
                                                start=True, stop=True)
                    last.then_inc(y_done, 1)

            def chunk(c, x, n):
                for s in range(TILES * STEPS):
                    t, b = divmod(s, STEPS)
                    gram_step(c, x, t, b)
                    if b in TURN_AT:
                        if t < TILES - 1:
                            turn_step(c, t + 1, TURN_AT[b])
                        elif not is_last(c):
                            turn_step(c + 1, 0, TURN_AT[b])
                    if s in HOT_AT and not is_last(c):
                        hot_step(c + 1, HOT_AT[s])
                    if mlp_at(c, s):
                        mlp_item(c - 1, *mlp_at(c, s))
                if not is_last(c):
                    triangle(c)
                if is_first(c):
                    pe.wait_ge(w_ready, W_ITEMS)
                    pe.wait_ge(ones_ready, 1)
                    pe.wait_ge(blanks_ready, 5)

            for q in range(NH):
                hot_step(0, 2 * q)
                hot_step(0, 2 * q + 1)
                if q == FIRST_TURN:
                    pe.wait_ge(ident_ready, 1)
                if q >= FIRST_TURN:
                    turn_step(0, 0, q - FIRST_TURN)
            pe.wait_ge(blanks_ready, 3)
            all_chunks(pe, chunk)
            finish(mlp_item, lambda c, x: None, triangle)
            pe.wait_ge(y_ready, CHUNKS)
            nc.tensor.transpose(ps_m[0:CHUNKS * TILES, 1, 0:P], y_all[:, :], ident[:, :]).then_inc(y_turned, 1)

        @block.scalar
        def _(act):
            def hot_evac(c, x, q, body=None):
                act.wait_ge(onehot_used, HALVES * c + 2 * q + 2)
                if q == 0 and body is not None and is_first(body):
                    act.wait_ge(hot_ready, NH)
                    act.wait_ge(onehot_ready, HALVES)
                if q == 0:
                    act.wait_ge(dense_x_loaded, 16 * (c + 1))
                    if body is not None and not is_first(body):
                        act.wait_ge(zd_ready, body)
                    for t in range(TILES):
                        nc.scalar.copy(x_tile(x, t)[:, :, 0].rearrange("p (g j) -> p g j", j=J),
                                       dense_x[:, :].rearrange("p (j g) -> p g j", j=J)[:, GT * t:GT * (t + 1), :]
                                       ).then_inc(dense_in_x, 1)
                nc.scalar.copy(X[:, x, :].rearrange("p (s n) -> p s n", n=NS)[:, :, 1 + q],
                               ps_hot[:, 0:CHUNK]).then_inc(hot_in_x, 1)

            def turn_evac(c, x, t, b):
                act.wait_ge(xt_done, TB * (TILES * c + t) + b + 1)
                n0, n = 1 + NH + GB * b, min(GB, NC - GB * b)
                nc.scalar.copy(x_tile(x, t)[:, :, n0:n0 + n],
                               ps_xt[:, (TB * t + b) % 2, 0:n * P].rearrange("p (n s) -> p s n", n=n)
                               ).then_inc(xt_in_x, 1)

            def gram_evac(c, t, b):
                act.wait_ge(gram_done, STEPS * (TILES * c + t) + b + 1)
                g0 = GT * t + GG * b
                for j in range(J):
                    rows_j = slice(NS * j, min(NS * (j + 1), GM))
                    last = nc.scalar.copy(
                        G[rows_j, :, g0:g0 + GG],
                        ps_g[rows_j, b % 2, 0:GG * J * NM]
                        .rearrange("p (i m) -> p m i", i=GG)[:, NM * j:NM * (j + 1), :])
                last.then_inc(gram_in_g, 1)

            def mlp_item(u, what, i):
                bank = mlp_bank(u, what, i)
                if what == "z":
                    act.wait_ge(z_done, 2 * u + i + 1)
                    for dst, src in z_parts(u, i, z_hi):
                        last = nc.scalar.copy(dst, src)
                    last.then_inc(z_hi_ready, 1)
                elif what == "h1":
                    act.wait_ge(h1_done, M1 * u + i + 1)
                    if i >= 2:
                        act.wait_ge(h1_ready, M1 * u + i - 1)
                    nc.scalar.activation(h1_f[:, i % 2, :], bank[:, 0:CHUNK], ACT.Relu,
                                         bias=b1_sb[:, i:i + 1]).then_inc(h1_f_ready, 1)
                    act.wait_ge(h1_f_ready, M1 * u + i + 1)
                    nc.scalar.copy(h1_hi[:, i, :], h1_f[:, i % 2, :]).then_inc(h1_hi_ready, 1)
                elif what == "h2":
                    act.wait_ge(h2_done, M2 * u + i + 1)
                    nc.scalar.activation(h2[:, i, :], bank[:, 0:CHUNK], ACT.Relu,
                                         bias=b2_sb[:, i:i + 1]).then_inc(h2_ready, 1)

            def w_item(i):
                if i == 0:
                    act.wait_ge(wd_ready, 1)
                else:
                    act.wait_ge(w_loaded[i], 16)
                nc.scalar.copy(w_place(w1_hi, w2_hi, i), w_raw[i]).then_inc(w_hi_ready, 1)
                if i in (1, 2, 3):
                    act.wait_ge(w_ready, i)
                    for later in ((2, 3), (4,), (5,))[i - 1]:
                        load_w(act, later)

            def pack(c):
                for i in (1, 3):
                    act.wait_ge(tri_done, len(TRI) * c + i + 1)
                    pack_triangle(nc.scalar.copy, c, i).then_inc(zt_act, 1)

            def dense_to_z(c, x):
                if not is_first(c):
                    act.wait_ge(h1_done, M1 * c)
                nc.scalar.copy(split_samples(z_hi[:, ZK, :]), dense_of(x)).then_inc(zd_hi_ready, 1)

            def chunk(c, x, n):
                if not is_first(c):
                    act.wait_ge(tri_done, len(TRI) * c)
                for s in range(TILES * STEPS):
                    t, b = divmod(s, STEPS)
                    gram_evac(c, t, b)
                    if b in TURN_AT:
                        if t < TILES - 1:
                            turn_evac(c, x, t + 1, TURN_AT[b])
                        elif not is_last(c):
                            turn_evac(c + 1, 1 - x, 0, TURN_AT[b])
                    if s in HOT_AT and HOT_AT[s] % 2 == 1 and not is_last(c):
                        hot_evac(c + 1, 1 - x, HOT_AT[s] // 2, c)
                    if s in W_AT and is_first(c):
                        w_item(W_AT[s])
                    if mlp_at(c, s):
                        mlp_item(c - 1, *mlp_at(c, s))
                    if s == DENSE_AT and not is_last(c):
                        dense_to_z(c, x)
                if is_first(c):
                    act.wait_ge(blanks_ready, 5)
                if not is_last(c):
                    pack(c)

            def load_table(q):
                act.dma_start(hot_raw[0:KP, q, :], hot_tables[q].rearrange("(p k) d -> p (k d)", k=KT)
                              ).then_inc(hot_loaded[q], 16)

            def hot_hi(q):
                act.wait_ge(hot_loaded[q], 16)
                nc.scalar.copy(tab_hi[0:KP, q, :, :].rearrange("p k d -> p (k d)"), hot_raw[0:KP, q, :]
                               ).then_inc(hot_hi_ready, 1)
                if q + AHEAD < NH:
                    load_table(q + AHEAD)

            act.wait_ge(iota_ready, 1)
            nc.scalar.copy(row_no[:, :], row_no_i[:, :]).then_inc(row_no_ready, 1)
            for q in range(AHEAD):
                load_table(q)
            hot_hi(0)
            hot_hi(1)
            for q in range(NH):
                if q + 2 < NH:
                    hot_hi(q + 2)
                hot_evac(0, 0, q)
                if q >= FIRST_TURN:
                    turn_evac(0, 0, 0, q - FIRST_TURN)
            act.wait_ge(small_loaded, 48)
            all_chunks(act, chunk)
            finish(mlp_item, dense_to_z, pack)

        @block.vector
        def _(dve):
            def onehot_columns(ids, part):
                for k in range(HALF):
                    kk = part * HALF + k
                    last = nc.vector.tensor_scalar(onehot[0:KP, part, k, :], ids, row_no[0:KP, kk:kk + 1], None,
                                                   ALU.is_equal)
                last.then_inc(onehot_ready, 1)

            def make_onehot(c, x, n, half):
                q, part = half // 2, half % 2
                slot, count = ids_slot(x, n, q)
                if part == 0:
                    dve.wait_ge(ids_loaded[slot], 16 * count)
                    nc.vector.tensor_copy(ps_ids[0:KP, slot, :], ids_b[0:KP, slot, :]).then_inc(ids_used, 1)
                    dve.wait_ge(ids_used, NH * (c - 1) + q + 1)
                dve.wait_ge(onehot_used, HALVES * c + half - 1)
                onehot_columns(ps_ids[0:KP, slot, :], part)

            def mlp_item(u, what, i):
                if what == "z":
                    dve.wait_ge(z_hi_ready, 2 * u + i + 1)
                    for (lo, src), (hi, _) in zip(z_parts(u, i, z_lo), z_parts(u, i, z_hi)):
                        last = nc.vector.tensor_tensor(lo, src, hi, ALU.subtract)
                    last.then_inc(z_ready, 1)
                elif what == "h1":
                    dve.wait_ge(h1_hi_ready, M1 * u + i + 1)
                    nc.vector.tensor_tensor(h1_lo[:, i, :], h1_f[:, i % 2, :], h1_hi[:, i, :],
                                            ALU.subtract).then_inc(h1_ready, 1)
                elif what == "h2":
                    dve.wait_ge(h2_ready, M2 * u + i + 1)
                    if i == 0:
                        nc.vector.tensor_scalar(hw[:, :], h2[:, 0, :], w3_sb[:, 0:1], None, ALU.mult
                                                ).then_inc(hw_first, 1)
                    else:
                        dve.wait_ge(hw_first, u + 1)
                        nc.vector.scalar_tensor_tensor(hw[:, :], h2[:, i, :], w3_sb[:, i:i + 1], hw[:, :],
                                                       ALU.mult, ALU.add).then_inc(hw_ready, 1)
                else:
                    dve.wait_ge(y_done, u + 1)
                    nc.vector.tensor_copy(y_all[:, bass.ds(TILES * u, TILES)],
                                          mlp_bank(u, "y", 0)[:, 0:TILES]).then_inc(y_ready, 1)

            def add_dense_weights():
                dve.wait_ge(w_loaded[0], 32)
                nc.vector.tensor_tensor(w_raw[0], w_raw[0], h2_stage, ALU.add).then_inc(wd_ready, 1)

            def w_item(i):
                if i == 0:
                    dve.wait_ge(wd_ready, 1)
                dve.wait_ge(w_hi_ready, i + 1)
                nc.vector.tensor_tensor(w_place(w1_lo, w2_lo, i), w_raw[i], w_place(w1_hi, w2_hi, i),
                                        ALU.subtract).then_inc(w_ready, 1)
                if i == W_ITEMS - 1:
                    dve.wait_ge(w_ready, W_ITEMS)
                    nc.vector.memset(Zt[:, :, :], 0.0).then_inc(blanks_ready, 1)
                    dve.wait_ge(blanks_ready, 5)

            def dense_to_z(c, x):
                dve.wait_ge(zd_hi_ready, c + 1)
                nc.vector.tensor_tensor(split_samples(z_lo[:, ZK, :]), dense_of(x),
                                        split_samples(z_hi[:, ZK, :]), ALU.subtract).then_inc(zd_ready, 1)

            def pack(c):
                for i in (0, 2):
                    dve.wait_ge(tri_done, len(TRI) * c + i + 1)
                    pack_triangle(nc.vector.tensor_copy, c, i).then_inc(zt_dve, 1)

            def chunk(c, x, n):
                if not is_last(c):
                    make_onehot(c + 1, x, n, 0)
                    make_onehot(c + 1, x, n, 1)
                if not is_first(c):
                    pack(c - 1)
                for s in range(TILES * STEPS):
                    if HOT_AT.get(s + 2, 0) >= 2 and not is_last(c):
                        make_onehot(c + 1, x, n, HOT_AT[s + 2])
                    if is_first(c) and s == 0:
                        add_dense_weights()
                    if is_first(c) and s - 1 in W_AT:
                        w_item(W_AT[s - 1])
                    if mlp_at(c, s):
                        mlp_item(c - 1, *mlp_at(c, s))
                    if s == DENSE_AT and not is_last(c):
                        dense_to_z(c, x)

            def clear_blanks(x):
                nc.vector.memset(X[:, x, :].rearrange("p (s n) -> p s n", n=NS)[:, :, NV:NS], 0.0
                                 ).then_inc(blanks_ready, 1)

            def split_table(q):
                dve.wait_ge(hot_hi_ready, q + 1)
                nc.vector.tensor_tensor(tab_lo[0:KP, q, :, :].rearrange("p k d -> p (k d)"), hot_raw[0:KP, q, :],
                                        tab_hi[0:KP, q, :, :].rearrange("p k d -> p (k d)"),
                                        ALU.subtract).then_inc(hot_ready, 1)

            nc.vector.memset(ones[:, :], 1.0).then_inc(ones_ready, 1)
            nc.vector.memset(z_hi[0:K3, 2, :].bitcast(F32), 0.0).then_inc(blanks_ready, 1)
            nc.vector.memset(z_lo[0:K3, 2, :].bitcast(F32), 0.0).then_inc(blanks_ready, 1)
            clear_blanks(0)
            dve.wait_ge(row_no_ready, 1)
            for q in range(NH):
                if q > 0:
                    split_table(q)
                for part in range(2):
                    for i, (q0, _) in enumerate(FIRST_IDS):
                        if q == q0 and part == 0:
                            dve.wait_ge(ids_first_loaded[i], 16)
                    if q > 0:
                        dve.wait_ge(onehot_used, 2 * q + part - 1)
                    ids = ids_first_x[0:KP, q, :] if q < IN_X else ids_first_g[0:KP, q - IN_X, :]
                    onehot_columns(ids, part)
                if q == 0:
                    split_table(q)
            dve.wait_ge(hot_ready, NH)
            dve.wait_ge(onehot_ready, HALVES)
            clear_blanks(1)
            dve.wait_ge(small_loaded, 48)
            all_chunks(dve, chunk)
            finish(mlp_item, dense_to_z, pack)
            dve.wait_ge(y_turned, 1)
            nc.vector.tensor_copy(y_sb[:, :], ps_m[0:CHUNKS * TILES, 1, 0:P]).then_inc(y_sb_ready, 1)


def kernel(**inputs):
    import numpy as np
    import concourse.bacc as bacc
    from concourse.bass_utils import run_bass_kernel_spmd

    a = {n: np.asarray(v) for n, v in inputs.items()}
    ids = a["ids"].reshape(CHUNKS, J, TILES, GT, NT)
    idx = np.ascontiguousarray(ids[..., list(COLD)].transpose(3, 1, 0, 2, 4)).reshape(P, CHUNKS * TILES, NC)
    ids_rows = np.ascontiguousarray(ids[..., list(HOT)].transpose(0, 4, 2, 3, 1)).reshape(CHUNKS, NH, CHUNK)
    w1 = a["W_top1"]
    w1_pairs = np.zeros((ZK * P, H1), w1.dtype)
    w1_pairs[0:P] = w1[[w1_row(p) for p in ODD[:P]]]
    w1_pairs[P:2 * P] = w1[[w1_row(p) for p in EVEN[:P]]]
    w1_pairs[2 * P:2 * P + REST_ODD] = w1[[w1_row(p) for p in ODD[P:]]]
    w1_pairs[2 * P + UP:2 * P + K3] = w1[[w1_row(p) for p in EVEN[P:]]]
    arrays = {
        "idx": idx,
        "ids_rows": ids_rows,
        "dense_t": np.ascontiguousarray(a["r_dense_proj"].T),
        "w1_pairs": w1_pairs,
        "w1_dense": np.ascontiguousarray(np.concatenate([w1[0:D], w1[D + NPAIR:]])),
        "b1": a["b_top1"], "w2": a["W_top2"], "b2": a["b_top2"], "w3": a["W_top3"],
    }
    for t in HOT + COLD:
        arrays[f"tbl_{t}"] = a[f"tbl_{t}"]

    nc = bacc.Bacc("TRN2", target_bir_lowering=False, num_devices=1)
    ap = {n: nc.dram_tensor(n, v.shape, mybir.dt.from_np(v.dtype), kind="ExternalInput").ap()
          for n, v in arrays.items()}
    out = nc.dram_tensor("out", (BATCH, 1), F32, kind="ExternalOutput").ap()
    dlrm_kernel(nc, ap["idx"], ap["ids_rows"], ap["dense_t"], [ap[f"tbl_{t}"] for t in HOT],
                [ap[f"tbl_{t}"] for t in COLD], ap["w1_pairs"], ap["w1_dense"], ap["b1"], ap["w2"], ap["b2"],
                ap["w3"], out)
    r = run_bass_kernel_spmd(nc, [arrays], core_ids=[0])
    return r.results[0]["out"]
```
